# Optimizing a Trainium2 kernel written in Bass

```python
import numpy as np
import jax
import jax.numpy as jnp

def _softmax(x, axis=-1):
    return jax.nn.softmax(x, axis=axis)

def _gelu(x):
    return jax.nn.gelu(x, approximate=True)

def _silu(x):
    return jax.nn.silu(x)

def _sigmoid(x):
    return jax.nn.sigmoid(x)

def _layernorm(x, axis=-1, eps=1e-05):
    m = jnp.mean(x, axis=axis, keepdims=True)
    v = jnp.var(x, axis=axis, keepdims=True)
    return (x - m) / jnp.sqrt(v + eps)

def _scatter_add(tgt, idx, src, axis=0):
    return tgt.at[idx].add(src)

def _segment_sum(src, seg, n):
    return jax.ops.segment_sum(src, seg, n)
kernel_name = 'mk_seq_preln_d1_jaxref_r4_8e2243'

def setup_inputs(seed: int=0):
    np.random.seed(seed)
    _w = jnp.asarray

    def _L0_attn_setup():
        import jax, jax.numpy as jnp
        import numpy as np
        B, S, H, NH, MRP = (4, 256, 256, 16, 64)
        DK = H // NH
        VOCAB = 2 * MRP + 1

        def _rel_idx(seq_len):
            r = jnp.arange(seq_len)
            dist = r[None, :] - r[:, None]
            return jnp.clip(dist, -MRP, MRP) + MRP
        key = jax.random.key(seed)
        ks = jax.random.split(key, 12)
        sc = 1.0 / np.sqrt(H)
        inp = {'x': jax.random.normal(ks[0], (B, S, H), jnp.float32), 'mask': jnp.ones((B, S), jnp.int32), 'Wq': jax.random.normal(ks[1], (H, H), jnp.float32) * sc, 'bq': jnp.zeros((H,), jnp.float32), 'Wk': jax.random.normal(ks[2], (H, H), jnp.float32) * sc, 'bk': jnp.zeros((H,), jnp.float32), 'Wv': jax.random.normal(ks[3], (H, H), jnp.float32) * sc, 'bv': jnp.zeros((H,), jnp.float32), 'Wo': jax.random.normal(ks[4], (H, H), jnp.float32) * sc, 'bo': jnp.zeros((H,), jnp.float32), 'embK': jax.random.normal(ks[5], (VOCAB, DK), jnp.float32), 'embV': jax.random.normal(ks[6], (VOCAB, DK), jnp.float32)}
        return inp
    _L0_attn_in = _L0_attn_setup()

    def _L0_ffn_setup():
        import jax, jax.numpy as jnp
        import numpy as np
        D = 256
        H = 16
        DK = D // H
        E = 8
        DFF = 4 * D
        TOPK = 2
        EPS = 1e-05

        def _layernorm(x, g, b):
            m = jnp.mean(x, axis=-1, keepdims=True)
            v = jnp.mean(jnp.square(x - m), axis=-1, keepdims=True)
            return (x - m) * jax.lax.rsqrt(v + EPS) * g + b
        key = jax.random.key(seed)
        ks = jax.random.split(key, 16)
        s_in = 1.0 / np.sqrt(D)
        s_ff = 1.0 / np.sqrt(DFF)
        return {'x': jax.random.normal(ks[0], (2, 512, D), dtype=jnp.float32), 'ln1_g': jnp.ones((D,), jnp.float32), 'ln1_b': jnp.zeros((D,), jnp.float32), 'w_qkv': jax.random.normal(ks[1], (D, 3 * D), jnp.float32) * s_in, 'b_qkv': jnp.zeros((3 * D,), jnp.float32), 'w_o': jax.random.normal(ks[2], (D, D), jnp.float32) * s_in, 'b_o': jnp.zeros((D,), jnp.float32), 'ln2_g': jnp.ones((D,), jnp.float32), 'ln2_b': jnp.zeros((D,), jnp.float32), 'gate_w': jax.random.normal(ks[3], (D, E), jnp.float32) * s_in, 'gate_b': jnp.zeros((E,), jnp.float32), 'W1': jax.random.normal(ks[4], (E, D, DFF), jnp.float32) * s_in, 'b1': jnp.zeros((E, DFF), jnp.float32), 'W2': jax.random.normal(ks[5], (E, DFF, D), jnp.float32) * s_ff, 'b2': jnp.zeros((E, D), jnp.float32)}
    _L0_ffn_in = _L0_ffn_setup()
    _d = {'L0_attn_x': _L0_attn_in['x'], 'L0_attn_mask': _L0_attn_in['mask'], 'L0_attn_Wq': _L0_attn_in['Wq'], 'L0_attn_bq': _L0_attn_in['bq'], 'L0_attn_Wk': _L0_attn_in['Wk'], 'L0_attn_bk': _L0_attn_in['bk'], 'L0_attn_Wv': _L0_attn_in['Wv'], 'L0_attn_bv': _L0_attn_in['bv'], 'L0_attn_Wo': _L0_attn_in['Wo'], 'L0_attn_bo': _L0_attn_in['bo'], 'L0_attn_embK': _L0_attn_in['embK'], 'L0_attn_embV': _L0_attn_in['embV'], 'L0_ffn_ln1_g': _L0_ffn_in['ln1_g'], 'L0_ffn_ln1_b': _L0_ffn_in['ln1_b'], 'L0_ffn_w_qkv': _L0_ffn_in['w_qkv'], 'L0_ffn_b_qkv': _L0_ffn_in['b_qkv'], 'L0_ffn_w_o': _L0_ffn_in['w_o'], 'L0_ffn_b_o': _L0_ffn_in['b_o'], 'L0_ffn_ln2_g': _L0_ffn_in['ln2_g'], 'L0_ffn_ln2_b': _L0_ffn_in['ln2_b'], 'L0_ffn_gate_w': _L0_ffn_in['gate_w'], 'L0_ffn_gate_b': _L0_ffn_in['gate_b'], 'L0_ffn_W1': _L0_ffn_in['W1'], 'L0_ffn_b1': _L0_ffn_in['b1'], 'L0_ffn_W2': _L0_ffn_in['W2'], 'L0_ffn_b2': _L0_ffn_in['b2']}
    _x0 = _d['L0_attn_x']
    _d['L0_attn_x'] = jax.random.normal(jax.random.fold_in(jax.random.key(seed), 1), (2, 2048, 256), dtype=_x0.dtype)
    del _x0
    return _d

def reference(L0_attn_x, L0_attn_mask, L0_attn_Wq, L0_attn_bq, L0_attn_Wk, L0_attn_bk, L0_attn_Wv, L0_attn_bv, L0_attn_Wo, L0_attn_bo, L0_attn_embK, L0_attn_embV, L0_ffn_ln1_g, L0_ffn_ln1_b, L0_ffn_w_qkv, L0_ffn_b_qkv, L0_ffn_w_o, L0_ffn_b_o, L0_ffn_ln2_g, L0_ffn_ln2_b, L0_ffn_gate_w, L0_ffn_gate_b, L0_ffn_W1, L0_ffn_b1, L0_ffn_W2, L0_ffn_b2):

    def _L0_attn_ref(x, mask, Wq, bq, Wk, bk, Wv, bv, Wo, bo, embK, embV):
        import jax, jax.numpy as jnp
        import numpy as np
        B, S, H, NH, MRP = (4, 256, 256, 16, 64)
        DK = H // NH
        VOCAB = 2 * MRP + 1

        def _rel_idx(seq_len):
            r = jnp.arange(seq_len)
            dist = r[None, :] - r[:, None]
            return jnp.clip(dist, -MRP, MRP) + MRP
        nb, seq_len, _ = x.shape
        idx = _rel_idx(seq_len)
        rk = embK[idx]
        rv = embV[idx]

        def proj(W, b):
            return (x @ W.T + b).reshape(nb, seq_len, NH, DK).transpose(0, 2, 1, 3)
        q = proj(Wq, bq)
        k = proj(Wk, bk)
        v = proj(Wv, bv)
        logits = jnp.einsum('bhqd,bhkd->bhqk', q, k) + jnp.einsum('bhqd,qkd->bhqk', q, rk)
        w = jax.nn.softmax(logits, axis=-1)
        out = jnp.einsum('bhqk,bhkd->bhqd', w, v) + jnp.einsum('bhqk,qkd->bhqd', w, rv)
        out = out.transpose(0, 2, 1, 3).reshape(nb, seq_len, NH * DK)
        return out @ Wo.T + bo

    def _L0_ffn_ref(x, ln1_g, ln1_b, w_qkv, b_qkv, w_o, b_o, ln2_g, ln2_b, gate_w, gate_b, W1, b1, W2, b2):
        import jax, jax.numpy as jnp
        import numpy as np
        D = 256
        H = 16
        DK = D // H
        E = 8
        DFF = 4 * D
        TOPK = 2
        EPS = 1e-05

        def _layernorm(x, g, b):
            m = jnp.mean(x, axis=-1, keepdims=True)
            v = jnp.mean(jnp.square(x - m), axis=-1, keepdims=True)
            return (x - m) * jax.lax.rsqrt(v + EPS) * g + b
        B, S, _ = x.shape
        h = _layernorm(x, ln1_g, ln1_b)
        qkv = h @ w_qkv + b_qkv
        q, k, v = jnp.split(qkv, 3, axis=-1)
        q = q.reshape(B, S, H, DK)
        k = k.reshape(B, S, H, DK)
        v = v.reshape(B, S, H, DK)
        scores = jnp.einsum('bqhd,bkhd->bhqk', q, k) / np.sqrt(DK)
        attn = jax.nn.softmax(scores, axis=-1)
        o = jnp.einsum('bhqk,bkhd->bqhd', attn, v).reshape(B, S, D)
        x = x + o @ w_o + b_o
        h = _layernorm(x, ln2_g, ln2_b).reshape(B * S, D)
        logits = h @ gate_w + gate_b
        topv, topi = jax.lax.top_k(logits, TOPK)
        gw = jax.nn.softmax(topv, axis=-1)
        ew = jnp.sum(jax.nn.one_hot(topi, E, dtype=h.dtype) * gw[..., None], axis=1)
        hid = jax.nn.relu(jnp.einsum('td,edf->etf', h, W1) + b1[:, None, :])
        out_e = jnp.einsum('etf,efd->etd', hid, W2) + b2[:, None, :]
        moe = jnp.einsum('etd,te->td', out_e, ew)
        return x + moe.reshape(B, S, D)
    x = L0_attn_x
    x = x + _L0_attn_ref(_layernorm(x, axis=-1), L0_attn_mask, L0_attn_Wq, L0_attn_bq, L0_attn_Wk, L0_attn_bk, L0_attn_Wv, L0_attn_bv, L0_attn_Wo, L0_attn_bo, L0_attn_embK, L0_attn_embV)
    x = x + _L0_ffn_ref(_layernorm(x, axis=-1), L0_ffn_ln1_g, L0_ffn_ln1_b, L0_ffn_w_qkv, L0_ffn_b_qkv, L0_ffn_w_o, L0_ffn_b_o, L0_ffn_ln2_g, L0_ffn_ln2_b, L0_ffn_gate_w, L0_ffn_gate_b, L0_ffn_W1, L0_ffn_b1, L0_ffn_W2, L0_ffn_b2)
    return x

_drawn_inputs = setup_inputs


def setup_inputs(seed=0):
    import zlib

    import numpy as np

    out = dict(_drawn_inputs(seed))
    spreads = {'L0_attn_bq': (0.0, 0.1),
     'L0_attn_bk': (0.0, 0.8),
     'L0_attn_bv': (0.0, 0.1),
     'L0_attn_bo': (0.0, 0.1),
     'L0_ffn_ln1_g': (1.0, 0.2),
     'L0_ffn_ln1_b': (0.0, 0.1),
     'L0_ffn_b_qkv': (0.0, 0.1),
     'L0_ffn_b_o': (0.0, 0.1),
     'L0_ffn_ln2_g': (1.0, 0.2),
     'L0_ffn_ln2_b': (0.0, 0.1),
     'L0_ffn_gate_b': (0.0, 0.1),
     'L0_ffn_b1': (0.0, 0.371),
     'L0_ffn_b2': (0.0, 0.271)}
    factors = {}
    for name, (base, spread) in spreads.items():
        noise = np.random.default_rng([zlib.crc32(name.encode()), seed]).standard_normal(out[name].shape)
        drawn = base * np.exp(spread * noise) if base else spread * noise
        out[name] = jnp.asarray(drawn.astype(out[name].dtype))
    for name, factor in factors.items():
        out[name] = (out[name] * factor).astype(out[name].dtype)
    return out
```

```python
import numpy as np
import concourse.bass as bass
import concourse.mybir as mybir
from contextlib import ExitStack

F32 = mybir.dt.float32
BF16 = mybir.dt.bfloat16
ACT = mybir.ActivationFunctionType
ALU = mybir.AluOpType
AX = mybir.AxisListType

P = 128
D = 256
CH = D // P
NH = 16
DK = D // NH
NB = 2
S = 2048
T = NB * S
NT = S // P
MRP = 64
NE = 8
DFF = 4 * D
FC = DFF // P
G = 512
TPG = G // P
NG = T // G
EPS = 1e-5
Q_PART = (0, 0, 0, 1, 1, 2)
K_PART = (0, 1, 2, 0, 1, 0)
KR = len(Q_PART) * DK
NM = 3


def ready(engine, value):
    return value if isinstance(value, int) else engine.snap(value)


def bcast_rows(ap, n=P):
    return bass.AP(ap.tensor, ap.offset, [[0, n]] + [list(x) for x in ap.ap])


class Sem:

    def __init__(self, ctx, nc, name, credit):
        self.h = ctx.enter_context(nc.semaphore(name))
        self.credit = credit

    def wait(self, engine, n):
        if not isinstance(n, int) or n > 0:
            engine.wait_ge(self.h, n + self.credit)


def wait_all(engine, *waits):
    waits = [(s, n if isinstance(n, int) else engine.to_reg(n + s.credit)) for s, n in waits]
    for s, n in waits:
        if not isinstance(n, int):
            engine.wait_ge(s.h, n)
        elif n > 0:
            engine.wait_ge(s.h, n + s.credit)


def clear_semaphores(nc, sems):
    with nc.Block() as blk:
        @blk.sync
        def _(sp):
            for s in sems:
                sp.sem_clear(s.h if isinstance(s, Sem) else s)


def give_credits(engine, sems):
    for s in sems:
        engine.sem_inc(s.h, s.credit)


def ident_and_ones(nc, ident):
    with ExitStack() as ctx:
        s_zero, s_ident = sems = [ctx.enter_context(nc.semaphore(n)) for n in ("s_zero", "s_ident")]
        ctx.callback(clear_semaphores, nc, sems)
        blk = ctx.enter_context(nc.Block())
        @blk.gpsimd
        def _(pool):
            pool.memset(ident[:, :], 0.0).then_inc(s_zero, 1)
            pool.wait_ge(s_zero, 1)
            pool.affine_select(out=ident[:, :], in_=ident[:, :], compare_op=ALU.not_equal, fill=1.0,
                               base=0, pattern=[[-1, P]], channel_multiplier=1).then_inc(s_ident, 1)
            pool.wait_ge(s_ident, 1)


def transposed_weight(nc, name, w_dram, out_sb, ident):
    with ExitStack() as ctx:
        raw = ctx.enter_context(nc.sbuf_tensor(name + "_raw", [P, CH, D], F32))
        ps = ctx.enter_context(nc.psum_tensor(name + "_ps", [P, CH, D], F32))
        s_load, s_tr, s_out = sems = [ctx.enter_context(nc.semaphore(name + n)) for n in ("_load", "_tr", "_out")]
        ctx.callback(clear_semaphores, nc, sems)
        blk = ctx.enter_context(nc.Block())

        @blk.sync
        def _(sp):
            sp.dma_start(raw[:, :, :], w_dram.rearrange("(a p) c -> p a c", p=P)).then_inc(s_load, 16)

        @blk.tensor
        def _(pe):
            pe.wait_ge(s_load, 16)
            for a in range(CH):
                for c in range(CH):
                    last = pe.transpose(ps[:, c, a * P:(a + 1) * P], raw[:, a, c * P:(c + 1) * P], ident[:, :])
            last.then_inc(s_tr, 1)

        @blk.vector
        def _(dve):
            dve.wait_ge(s_tr, 1)
            dve.tensor_copy(out_sb[:, :, :], ps[:, :, :]).then_inc(s_out, 1)
            dve.wait_ge(s_out, 1)


def ln_proj_stage(nc, mode, src, ident, weights, cols, v_bias, dram, gain=None, save_ln=None):
    two_ln = save_ln is not None
    NS = 2 if two_ln else 1
    attn = mode != "gate"
    units = cols if attn else []
    NU = len(units)
    with ExitStack() as ctx:
        def sb(name, shape, dt=F32):
            return ctx.enter_context(nc.sbuf_tensor(f"{mode}_{name}", shape, dt))

        def ps(name, shape):
            return ctx.enter_context(nc.psum_tensor(f"{mode}_{name}", shape, F32))

        sems = []

        def sem(name, credit=16):
            sems.append(Sem(ctx, nc, f"{mode}_{name}", credit))
            return sems[-1]

        x = sb("x", [P, 2, TPG, D])
        h = sb("h", [P, 2, NS, TPG, D])
        stats = sb("stats", [P, 2, NS, TPG, 6])
        moments = sb("moments", [P, 2, NS, 5, TPG])
        mean = sb("mean", [P, 2, NS, TPG])
        ve = sb("ve", [P, 2, NS, TPG])
        sd = sb("sd", [P, 2, NS, TPG])
        rs = sb("rs", [P, 2, NS, TPG])
        hT = sb("hT", [P, 2, CH, G])
        full, r1, r2 = (sb(n, [P, 2, G]) for n in ("full", "r1", "r2")) if attn else (None, None, None)
        parts = sb("parts", [P, 4, 3, G], BF16) if attn else None
        vout = sb("vout", [P, 2, TPG, D]) if attn else None
        psT = ps("psT", [P, CH, G])
        psU = ps("psU", [P, 2, G])
        psV = ps("psV", [P, 2, 2, D])
        s_x = [sem(f"s_x{i}") for i in range(2)]
        s_stat, s_sum, s_mean, s_var, s_ve, s_sd, s_rs, s_h = (sem(n) for n in
            ("s_stat", "s_sum", "s_mean", "s_var", "s_ve", "s_sd", "s_rs", "s_h"))
        s_f = [sem(f"s_f{i}") for i in range(2)]
        s_t, s_hT, s_u, s_full, s_hi, s_r1, s_mid, s_lo, s_v, s_vo = (sem(n) for n in
            ("s_t", "s_hT", "s_u", "s_full", "s_hi", "s_r1", "s_mid", "s_lo", "s_v", "s_vo"))
        s_po = [sem(f"s_po{i}") for i in range(4)]
        s_vd = [sem(f"s_vd{i}") for i in range(2)]
        if not attn:
            hT_all, gate = dram["hT_all"], dram["gate"]
            lg, s_lg, s_all = dram["logits"], sem("s_lg"), sem("s_all")
        ctx.callback(clear_semaphores, nc, sems)
        blk = ctx.enter_context(nc.Block())

        def slot(q, m):
            return (NU * q + m) % 4

        def stored(it, q, m):
            return NU * 2 // 4 * it + (NU * q + m) // 4

        src_v = src.rearrange("(g j p) c -> g p j c", p=P, j=TPG)

        @blk.sync
        def _(sp):
            give_credits(sp, sems)
            with sp.Fori(0, NG // 2) as it:
                for q in range(2):
                    g = 2 * it + q
                    s_h.wait(sp, NS * TPG * (2 * it + q - 1))
                    sp.dma_start(x[:, q, :, :], src_v[bass.ds(g, 1), :, :, :].rearrange("g p j c -> p (g j) c")
                                 ).then_inc(s_x[q].h, 16)
            s_x[0].wait(sp, 16 * NG // 2)
            s_x[1].wait(sp, 16 * NG // 2)

        @blk.vector
        def _(dve):
            with dve.Fori(0, NG // 2) as it:
                for q in range(2):
                    g = 2 * it + q
                    s_x[q].wait(dve, 16 * (it + 1))
                    for n in range(NS):
                        k = TPG * (NS * g + n)
                        data = x[:, q] if n == 0 else h[:, q, 0]
                        for j in range(TPG):
                            dve.bn_stats(stats[:, q, n, j, :], data[:, j, :]).then_inc(s_stat.h, 1)
                        st, mo = stats[:, q, n, :, :], moments[:, q, n, :, :]
                        s_stat.wait(dve, k + TPG)
                        for o, a, b, op in ((0, 1, 4, ALU.add), (1, 1, 4, ALU.subtract), (2, 2, 5, ALU.add)):
                            dve.tensor_tensor(out=mo[:, o, :], in0=st[:, :, a], in1=st[:, :, b], op=op
                                              ).then_inc(s_sum.h, 1)
                        s_sum.wait(dve, 3 * (NS * g + n + 1))
                        dve.tensor_scalar(mean[:, q, n, :], mo[:, 0, :], 0.5, None, ALU.mult).then_inc(s_mean.h, 1)
                        dve.scalar_tensor_tensor(out=mo[:, 3, :], in0=mo[:, 1, :], scalar=0.25, in1=mo[:, 1, :],
                                                 op0=ALU.mult, op1=ALU.mult).then_inc(s_mean.h, 1)
                        s_mean.wait(dve, 2 * (NS * g + n + 1))
                        dve.scalar_tensor_tensor(out=mo[:, 4, :], in0=mo[:, 2, :], scalar=1.0 / D, in1=mo[:, 3, :],
                                                 op0=ALU.mult, op1=ALU.add).then_inc(s_var.h, 1)
                        s_var.wait(dve, NS * g + n + 1)
                        dve.tensor_scalar_add(ve[:, q, n, :], mo[:, 4, :], EPS).then_inc(s_ve.h, 1)
                        s_sd.wait(dve, NS * g + n + 1)
                        dve.reciprocal(rs[:, q, n, :], sd[:, q, n, :]).then_inc(s_rs.h, 1)
                        s_rs.wait(dve, NS * g + n + 1)
                        if n == 0 and two_ln:
                            s_f[q].wait(dve, 16 * it)
                        if n == NS - 1:
                            s_t.wait(dve, CH * (g - 1))
                        for j in range(TPG):
                            dve.tensor_scalar(h[:, q, n, j, :], data[:, j, :], mean[:, q, n, j:j + 1],
                                              rs[:, q, n, j:j + 1], ALU.subtract, ALU.mult).then_inc(s_h.h, 1)
                        if n < NS - 1:
                            s_h.wait(dve, k + TPG)
                    for step in range(NU + 2 if NU else 0):
                        if step < NU:
                            m, n, w = step, NU * g + step, step % 2
                            _, bias, scale, _ = units[m]
                            s_u.wait(dve, n + 1)
                            s_hi.wait(dve, n - 1)
                            s_r1.wait(dve, n - 1)
                            dve.tensor_scalar(full[:, w, :], psU[:, w, :], bias, scale, ALU.add, ALU.mult
                                              ).then_inc(s_full.h, 1)
                        if 0 <= step - 1 < NU:
                            m, n, w = step - 1, NU * g + step - 1, (step - 1) % 2
                            s_full.wait(dve, n + 1)
                            s_hi.wait(dve, n + 1)
                            s_mid.wait(dve, n - 1)
                            s_lo.wait(dve, n - 1)
                            dve.tensor_tensor(out=r1[:, w, :], in0=full[:, w, :], in1=parts[:, slot(q, m), 0, :],
                                              op=ALU.subtract).then_inc(s_r1.h, 1)
                        if 0 <= step - 2 < NU:
                            m, n, w = step - 2, NU * g + step - 2, step % 2
                            s_mid.wait(dve, n + 1)
                            s_po[slot(q, m)].wait(dve, 16 * stored(it, q, m))
                            dve.tensor_tensor(out=parts[:, slot(q, m), 2, :], in0=r1[:, w, :],
                                              in1=parts[:, slot(q, m), 1, :], op=ALU.subtract).then_inc(s_lo.h, 1)
                    if attn:
                        for v in range(2):
                            s_v.wait(dve, 2 * g + v + 1)
                            if v == 0:
                                s_vd[q].wait(dve, 16 * it)
                            dve.tensor_tensor(out=vout[:, q, 2 * v:2 * v + 2, :], in0=psV[:, v, :, :],
                                              in1=v_bias[:, :].rearrange("p (a c) -> p a c", a=1).to_broadcast([P, 2, D]),
                                              op=ALU.add).then_inc(s_vo.h, 1)
                    else:
                        s_hT.wait(dve, CH * (g + 1))
                        dve.tensor_copy(hT_all[:, :, bass.ds(g * G, G)], hT[:, q, :, :]).then_inc(s_all.h, 1)
                        s_lg.wait(dve, g + 1)
                        dve.tensor_copy(lg[:, bass.ds(g * TPG, TPG), :], psU[:, 0, 0:TPG * NE].rearrange(
                            "p (j e) -> p j e", e=NE)).then_inc(s_vo.h, 1)
            s_vo.wait(dve, (2 if attn else 1) * NG)

        @blk.scalar
        def _(act):
            if two_ln:
                save_v = save_ln.rearrange("(g j p) c -> g p j c", p=P, j=TPG)
            if attn:
                v_v = dram["v"].rearrange("(g j p) c -> g p j c", p=P, j=TPG)
            with act.Fori(0, NG // 2) as it:
                for q in range(2):
                    g = 2 * it + q
                    for n in range(NS):
                        s_ve.wait(act, NS * g + n + 1)
                        act.activation(sd[:, q, n, :], ve[:, q, n, :], ACT.Sqrt).then_inc(s_sd.h, 1)
                    if two_ln:
                        s_h.wait(act, NS * TPG * g + TPG)
                        act.dma_start(save_v[bass.ds(g, 1), :, :, :].rearrange("g p j c -> p (g j) c"),
                                      h[:, q, 0, :, :]).then_inc(s_f[q].h, 16)
                    for c in range(CH):
                        s_t.wait(act, CH * g + c + 1)
                        if c == 0 and attn:
                            s_v.wait(act, 2 * (g - 1))
                        if c == 0 and not attn:
                            s_lg.wait(act, g - 1)
                            s_all.wait(act, g - 1)
                        dst = hT[:, q, c, :]
                        if gain is None:
                            act.activation(dst, psT[:, c, :], ACT.Copy).then_inc(s_hT.h, 1)
                        else:
                            act.activation(dst, psT[:, c, :], ACT.Identity, bias=gain[:, 1, c:c + 1],
                                           scale=gain[:, 0, c:c + 1]).then_inc(s_hT.h, 1)
                    for step in range(NU + 2 if NU else 0):
                        if step < NU:
                            m, n = step, NU * g + step
                            s_full.wait(act, n + 1)
                            s_po[slot(q, m)].wait(act, 16 * stored(it, q, m))
                            act.activation(parts[:, slot(q, m), 0, :], full[:, m % 2, :], ACT.Copy
                                           ).then_inc(s_hi.h, 1)
                        if 0 <= step - 1 < NU:
                            m, n = step - 1, NU * g + step - 1
                            s_r1.wait(act, n + 1)
                            act.activation(parts[:, slot(q, m), 1, :], r1[:, m % 2, :], ACT.Copy
                                           ).then_inc(s_mid.h, 1)
                        if 0 <= step - 2 < NU:
                            m, n = step - 2, NU * g + step - 2
                            dst, row = units[m][3]
                            s_hi.wait(act, n + 1)
                            s_mid.wait(act, n + 1)
                            s_lo.wait(act, n + 1)
                            act.dma_start(dst[:, row:row + P, bass.ds(g * G, G)].rearrange("a p t -> p a t"),
                                          parts[:, slot(q, m), :, :]).then_inc(s_po[slot(q, m)].h, 16)
                    if attn:
                        s_vo.wait(act, 2 * g + 2)
                        act.dma_start(v_v[bass.ds(g, 1), :, :, :].rearrange("g p j c -> p (g j) c"),
                                      vout[:, q, :, :]).then_inc(s_vd[q].h, 16)
            for q in range(2):
                if two_ln:
                    s_f[q].wait(act, 16 * NG // 2)
                if attn:
                    s_vd[q].wait(act, 16 * NG // 2)
            if attn:
                for w in range(4):
                    s_po[w].wait(act, 16 * NU * NG // 4)

        @blk.tensor
        def _(pe):
            with pe.Fori(0, NG // 2) as it:
                for q in range(2):
                    g = 2 * it + q
                    s_h.wait(pe, TPG * NS * (g + 1))
                    for c in range(CH):
                        s_hT.wait(pe, CH * (g - 1) + c + 1)
                        for j in range(TPG):
                            last = pe.transpose(psT[:, c, j * P:(j + 1) * P],
                                                h[:, q, NS - 1, j, c * P:(c + 1) * P], ident[:, :])
                        last.then_inc(s_t.h, 1)
                    s_hT.wait(pe, CH * (g + 1))
                    for m, (col, _, _, _) in enumerate(units):
                        n = NU * g + m
                        s_full.wait(pe, n - 1)
                        for c in range(CH):
                            last = pe.matmul(psU[:, m % 2, :], weights[:, c, col:col + P], hT[:, q, c, :],
                                             start=c == 0, stop=c == CH - 1)
                        last.then_inc(s_u.h, 1)
                    if attn:
                        for v in range(2):
                            s_vo.wait(pe, 2 * (g - 1) + v + 1)
                            for i in range(2):
                                for c in range(CH):
                                    j = 2 * v + i
                                    last = pe.matmul(psV[:, v, i, :], hT[:, q, c, j * P:(j + 1) * P],
                                                     weights[:, c, 2 * D:3 * D], start=c == 0, stop=c == CH - 1)
                            last.then_inc(s_v.h, 1)
                    else:
                        s_vo.wait(pe, g)
                        for j in range(TPG):
                            for c in range(CH):
                                last = pe.matmul(psU[:, 0, j * NE:(j + 1) * NE], hT[:, q, c, j * P:(j + 1) * P],
                                                 gate[:, c, :], start=c == 0, stop=c == CH - 1)
                        last.then_inc(s_lg.h, 1)
U = 4
HEADS = NB * NH
NROT = 15
NZ = 2 * NROT + 1
W = 2 * P


def attention_stage(nc, rel, ident, sel, qd, kd, vd, o_rows, rel_tabs=None):
    tag = "ra" if rel else "pa"
    nz = NZ if rel else NT
    zw = nz * P
    exp_scale = 1.0
    lead = 3
    ring = []
    if rel:
        ring += [("F", c, 0) for c in range(4)]
    for c in range(4):
        ring += [("E", c, j) for j in range(7 if rel else 8)]
        if rel:
            ring += [("W", c, 0)]
            if c % 2:
                ring += [("R", c - 1, 0), ("R", c, 0)]
    NR = len(ring)
    RPRO = 8 if rel else 0
    used = [k != "R" for k, _, _ in ring]
    use_no = [sum(used[:n]) for n in range(NR)]
    NUSE = sum(used)
    NP = 4
    place = {(k, c): n for n, (k, c, _) in enumerate(ring)}
    chunk_end = [place["W" if rel else "E", c] for c in range(4)]

    NSTEP = NR // 2
    EARLY = 64 * 5 // NSTEP

    def banks_until(step):
        return 64 * (step + 1) // NSTEP

    M_STEP = next(n for n in range(NSTEP) if banks_until(n) >= 64 - EARLY) + 1
    M_COPY = banks_until(M_STEP) - (64 - EARLY)
    F_STEP = 2

    def banks(c, j):
        if not rel:
            return [[(2 * j + e, 0, G)] for e in range(2)]
        every = [[(4 * c + 4 + z, 0, G)] for z in range(11)]
        every += [[(4 * c + 1 + z, 0, P * (z + 1)), (4 * c + 15 + z, P * (z + 1), G)] for z in range(3)]
        return every[2 * j:2 * j + 2]

    with ExitStack() as ctx:
        def sb(name, shape, dt=F32):
            return ctx.enter_context(nc.sbuf_tensor(f"{tag}_{name}", shape, dt))

        def ps(name, shape):
            return ctx.enter_context(nc.psum_tensor(f"{tag}_{name}", shape, F32))

        sems = []

        def sem(name, credit=64):
            sems.append(Sem(ctx, nc, f"{tag}_{name}", credit))
            return sems[-1]

        qs = sb("qs", [P, U, S], BF16)
        zs = sb("zs", [P, U, zw], BF16)
        vall = sb("vall", [P, NB, NT, D])
        vs = sb("vs", [P, 2, nz, 32])
        pr = sb("p", [P, NP, 2 * G])
        ot = sb("ot", [P, 2, S])
        pm = sb("pm", [P, 2, NT, 5])
        nm = sb("nm", [P, 2, NT])
        mhi = sb("mhi", [P, NT], BF16)
        mmid = sb("mmid", [P, NT], BF16)
        mres = sb("mres", [P, NT])
        mp_all = sb("mp", [P, P])
        mp = mp_all[:, 0:NM * NT].rearrange("p (m i) -> p m i", i=NT)
        mrow = sb("mrow", [NM * NT, P], BF16)
        rec = sb("rec", [P, NT])
        ob = sb("ob", [P, NT, U * DK])
        if rel:
            e_stack, ev, ev_side = rel_tabs["e_stack"], rel_tabs["ev"], rel_tabs["ev_side"]
            dr_r, dr_p = rel_tabs["dr_r"], rel_tabs["dr_p"]
            delta = sb("delta", [P, 2, NT, P])
            sw = sb("sw", [P, 2, NT, W])
            vraw = sb("vraw", [P, NT, DK])
            skp = sb("skp", [P, 2, NT, P])
        psS = ps("psS", [P, 2, 2 * G])
        psA = ps("psA", [P, 2, G])
        psO = ps("psO", [P, G])
        psF = ps("psF", [P, NT, 32])

        s_init = sem("s_init")
        s_qz = [sem(f"s_qz{i}") for i in range(U)]
        s_vall = sem("s_vall")
        s_v = sem("s_v")
        s_a, s_amax = sem("s_a"), sem("s_amax")
        s_m, s_mt, s_mr, s_mq = sem("s_m"), sem("s_mt"), sem("s_mr"), sem("s_mq")
        s_fl, s_cp, s_us = sem("s_fl"), sem("s_cp"), sem("s_us")
        s_ob = sem("s_ob")
        s_oev, s_fm, s_rec, s_nf = sem("s_oev"), sem("s_fm"), sem("s_rec"), sem("s_nf")
        if rel:
            s_sw, s_wm = sem("s_sw"), sem("s_wm")
            s_we = sem("s_we")
            s_pw = [sem(f"s_pw{c}") for c in range(4)]
            s_pr = [sem(f"s_pr{c}") for c in range(4)]
            s_rw = [sem(f"s_rw{c}") for c in range(4)]
            s_dr = [sem(f"s_dr{c}") for c in range(4)]
        ctx.callback(clear_semaphores, nc, sems)
        blk = ctx.enter_context(nc.Block())

        def head(t):
            n = t % HEADS
            return n // NH, n % NH

        NLD = 2 * 6 if not rel else 18

        def load_stacks(sp, t, p):
            b, h = head(t)
            slot = p % U
            row = ready(sp, h * DK)
            col = {lo: ready(sp, b * S + lo) for lo in ((0, 64) if rel else (0,))}
            s_us.wait(sp, NUSE * (t - 3))
            n = 0
            for part_of, dst, srcs in ((Q_PART, qs, [(qd, 0, S, 0)]),
                                       (K_PART, zs, [(kd[1], 64, S, 0), (kd[0], 0, S - 64, S - 64)] if rel
                                        else [(kd[0], 0, S, 0)])):
                for src, lo, hi, at in srcs:
                    for i, part in enumerate(part_of):
                        sp.dma_start(dst[i * DK:(i + 1) * DK, slot, at:at + hi - lo],
                                     src[part, bass.ds(row, DK), bass.ds(col[lo], hi - lo)]
                                     ).then_inc(s_qz[slot].h, 16)
                        n += 1
            assert n == NLD

        def skew(tab, t_par, side, i0, n, k0, k1):
            base = ((t_par * 2 + side) * NT + i0) * P * W + P + k0
            return bass.AP(tab.tensor, tab.offset + base, [[W - 1, P], [P * W, n], [1, k1 - k0]])

        def rows(tab, t_par, side, i0, n):
            base = ((t_par * 2 + side) * NT + i0) * P * W + (P if side == 0 else 0)
            return bass.AP(tab.tensor, tab.offset + base, [[W, P], [P * W, n], [1, P]])

        def window_pieces(c):
            i0 = 4 * c
            left = [(0, 0, 1, 64, P), (0, 1, 3, 0, P)] if c == 0 else [(0, i0, 4, 0, P)]
            right = [(1, i0, 3, 0, P), (1, NT - 1, 1, 0, 64)] if c == 3 else [(1, i0, 4, 0, P)]
            return left + right

        def write_p(sp, t, p):
            for c in range(4):
                wait_all(sp, (s_we, NT * t + 4 * c + 4),
                         (s_pr[c], 32 * (t - 1)))
                for side, i0, n, k0, k1 in window_pieces(c):
                    col = P if side == 0 else 0
                    sp.dma_start(skew(dr_p, p % 2, side, i0, n, k0, k1),
                                 sw[:, p % 2, i0:i0 + n, col + k0:col + k1]).then_inc(s_pw[c].h, 16)

        def read_p(sp, t, p):
            for c in range(4):
                np_ = len(window_pieces(c))
                wait_all(sp, (s_pw[c], 16 * np_ * (t + 1)),
                         (s_fl, RPRO + NR * t + c + 1))
                for side in range(2):
                    sp.dma_start(skp[:, side, 4 * c:4 * c + 4, :], rows(dr_p, p % 2, side, 4 * c, 4)
                                 ).then_inc(s_pr[c].h, 16)

        def trip_r(sp, t, p, c, n):
            src = pr[:, RING_P(n), :].rearrange("p (i s r) -> p i s r", i=4, s=2)
            wait_all(sp, (s_cp, n + 1),
                     (s_dr[c], DR(c) * (t - 1)))
            for side in range(2):
                sp.dma_start(rows(dr_r, p % 2, side, 4 * c, 4), src[:, :, side, :]).then_inc(s_rw[c].h, 16)
            wait_all(sp, (s_rw[c], 32 * (t + 1)),
                     (s_amax, 64 * (t - 1) + 16 * (c + 1)))
            for side, i0, m, k0, k1 in window_pieces(c):
                sp.dma_start(delta[:, side, i0:i0 + m, k0:k1], skew(dr_r, p % 2, side, i0, m, k0, k1)
                             ).then_inc(s_dr[c].h, 16)

        def DR(c):
            return 16 * len(window_pieces(c))

        def RING_P(n):
            return ring_static(n) % NP

        def ring_static(n):
            return n if isinstance(n, int) else n.position

        class At:
            def __init__(self, t, n):
                self.value = RPRO + NR * t + n
                self.position = RPRO + n

            def __add__(self, k):
                return self.value + k

        assert NR % NP == 0 and RPRO % NP == 0

        def send_m(sp, t, p):
            s_mr.wait(sp, t + 1)
            sp.dma_start(qs[KR:KR + NM, p % U, :], mrow[:, :]).then_inc(s_mq.h, 16)

        def store_o(sp, t):
            b, h = head(t + HEADS - U)
            row, col = ready(sp, b * S), ready(sp, h * DK)
            s_nf.wait(sp, t + 1)
            sp.dma_start(o_rows[bass.ds(row, S), bass.ds(col, U * DK)].rearrange("(i q) c -> q i c", q=P),
                         ob[:, :, :]).then_inc(s_ob.h, 16)

        @blk.sync
        def _(sp):
            give_credits(sp, sems)
            for b in range(NB):
                if rel:
                    sp.dma_start(vall[:, b, 0:NROT, :], vd[b * S + 64:b * S + 64 + NROT * P, :].rearrange(
                        "(z p) c -> p z c", p=P)).then_inc(s_vall.h, 16)
                    sp.dma_start(vall[0:64, b, NROT, :], vd[(b + 1) * S - 64:(b + 1) * S, :]).then_inc(s_vall.h, 16)
                    sp.dma_start(vall[64:P, b, NROT, :], vd[b * S:b * S + 64, :]).then_inc(s_vall.h, 16)
                else:
                    sp.dma_start(vall[:, b, :, :], vd[b * S:(b + 1) * S, :].rearrange(
                        "(z p) c -> p z c", p=P)).then_inc(s_vall.h, 16)
            for t in range(lead):
                load_stacks(sp, t, t)
            if rel:
                for t in range(2):
                    for c in range(4):
                        trip_r(sp, t, t, c, 4 * t + c)
            send_m(sp, 0, 0)
            with sp.Fori(0, HEADS // U) as it:
                for p in range(U):
                    t = U * it + p
                    if rel:
                        write_p(sp, t, p)
                    load_stacks(sp, t + lead, p + lead)
                    if rel:
                        read_p(sp, t, p)
                        for c in range(2):
                            trip_r(sp, t + 2, p + 2, c, At(t, place["R", c]))
                    if p == 0:
                        store_o(sp, t)
                    send_m(sp, t + 1, p + 1)
                    if rel:
                        for c in range(2, 4):
                            trip_r(sp, t + 2, p + 2, c, At(t, place["R", c]))
            for t in range(HEADS, HEADS + lead):
                s_qz[t % U].wait(sp, 16 * NLD * (t // U + 1))
            s_mq.wait(sp, 16 * (HEADS + 1))
            store_o(sp, HEADS)
            s_ob.wait(sp, 16 * (HEADS // U + 1))
            if rel:
                for c in range(4):
                    s_dr[c].wait(sp, DR(c) * (HEADS + 2))
                    s_pr[c].wait(sp, 32 * HEADS)

        NV = 5 if rel else 1
        NINIT = 9 if rel else 6

        def lay_v(pool, t, p):
            b, h = head(t)
            b, col = ready(pool, b), ready(pool, h * DK)
            s_us.wait(pool, NUSE * (t - 1))
            if not rel:
                pool.tensor_copy(vs[:, p % 2, :, 0:DK], vall[:, bass.ds(b, 1), :, bass.ds(col, DK)].rearrange(
                    "p b z d -> p (b z) d")).then_inc(s_v.h, 1)
                return
            s_v.wait(pool, NV * t)
            pool.tensor_copy(vraw[:, :, :], vall[:, bass.ds(b, 1), :, bass.ds(col, DK)].rearrange(
                "p b z d -> p (b z) d")).then_inc(s_v.h, 1)
            k = 1
            for side, z0 in ((1, 0), (0, NROT + 1)):
                s_v.wait(pool, NV * t + k)
                pool.tensor_tensor(out=vs[:, p % 2, z0:z0 + NROT, 0:DK],
                                   in0=vraw[:, 0:NROT, :],
                                   in1=ev_side[:, side, 0:NROT, :], op=ALU.add).then_inc(s_v.h, 1)
                k += 1
            for side, lo in ((1, 0), (0, 64)):
                s_v.wait(pool, NV * t + k)
                pool.tensor_tensor(out=vs[lo:lo + 64, p % 2, NROT, 0:DK],
                                   in0=vraw[lo:lo + 64, NROT, :],
                                   in1=ev_side[lo:lo + 64, side, 0, :], op=ALU.add).then_inc(s_v.h, 1)
                k += 1


        @blk.gpsimd
        def _(pool):
            s_vall.wait(pool, 16 * NB * (3 if rel else 1))
            s_init.wait(pool, NINIT)
            lay_v(pool, 0, 0)
            with pool.Fori(0, HEADS // U) as it:
                for p in range(U):
                    lay_v(pool, U * it + p + 1, p + 1)


        def amax(dve, t, p, u):
            i, k = u // 4, u % 4
            bank = psA[:, u % 2, :]
            if rel and k == 1 and i > 0:
                window_max(dve, t, p, i - 1)
            s_a.wait(dve, 64 * t + u + 1)
            lo, hi = 0, G
            if rel and k == 0:
                s_dr[i // 4].wait(dve, DR(i // 4) * (t + 1))
                if i % 4 == 0:
                    c = i // 4
                    s_we.wait(dve, NT * (t - 2) + 4 * c + 4)
                    s_pw[c].wait(dve, DR(c) * (t - 1))
                    s_us.wait(dve, NUSE * (t - 2) + use_no[chunk_end[c]] + 1)
            if rel and k in (0, 3):
                side = 1 if k == 0 else 0
                at = 0 if k == 0 else G - P
                col = P if side == 0 else 0
                lo, hi = (P, G) if k == 0 else (0, G - P)
                dve.tensor_tensor(out=sw[:, p % 2, i, col:col + P], in0=bank[:, at:at + P],
                                  in1=delta[:, side, i, :], op=ALU.add).then_inc(s_sw.h, 1)
            dve.reduce_max(pm[:, p % 2, i, k:k + 1], bank[:, lo:hi], AX.X).then_inc(s_amax.h, 1)

        def f_done(eng, t):
            if rel:
                s_us.wait(eng, NUSE * t + 4)
            else:
                s_fm.wait(eng, t + 1)

        def window_max(dve, t, p, i):
            s_sw.wait(dve, 2 * NT * t + 2 * i + 2)
            dve.reduce_max(pm[:, p % 2, i, 4:5], sw[:, p % 2, i, :], AX.X).then_inc(s_wm.h, 1)

        MS = 8

        def m_parts(dve, t, p):
            q = p % 2
            if rel:
                window_max(dve, t, p, NT - 1)
                s_wm.wait(dve, NT * (t + 1))
            s_amax.wait(dve, 64 * (t + 1))
            step = [0]

            def then(ins):
                step[0] += 1
                ins.then_inc(s_m.h, 1)
                if step[0] < MS:
                    s_m.wait(dve, MS * t + step[0])

            if rel:
                s_we.wait(dve, NT * (t - 1))
            s_mt.wait(dve, t)
            then(dve.reduce_max(mres[:, :], pm[:, q, :, 0:5 if rel else 4], AX.X))
            then(dve.tensor_scalar(nm[:, q, :], mres[:, :], -1.0, None, ALU.mult))
            then(dve.tensor_copy(mhi[:, :], nm[:, q, :]))
            then(dve.tensor_copy(mp[:, 0, :], mhi[:, :]))
            then(dve.tensor_tensor(out=mres[:, :], in0=nm[:, q, :], in1=mp[:, 0, :], op=ALU.subtract))
            then(dve.tensor_copy(mmid[:, :], mres[:, :]))
            then(dve.tensor_copy(mp[:, 1, :], mmid[:, :]))
            then(dve.tensor_tensor(out=mp[:, 2, :], in0=mres[:, :], in1=mp[:, 1, :], op=ALU.subtract))

        def m_copy(dve, t):
            s_mt.wait(dve, t + 1)
            s_mq.wait(dve, 16 * t)
            dve.tensor_copy(mrow[:, :], psF[0:NM * NT, 0:4, :].rearrange("p a b -> p (a b)")).then_inc(s_mr.h, 1)

        def divide(dve, t, p, stores_before):
            col = (p - 1) % U * DK
            if col == 0:
                s_ob.wait(dve, 16 * stores_before)
            f_done(dve, t)
            s_nf.wait(dve, t)
            dve.reciprocal(rec[:, :], psF[:, :, DK]).then_inc(s_rec.h, 1)
            s_rec.wait(dve, t + 1)
            dve.tensor_tensor(out=ob[:, :, col:col + DK], in0=psF[:, :, 0:DK],
                              in1=rec[:, :].rearrange("p (i a) -> p i a", a=1).to_broadcast([P, NT, DK]),
                              op=ALU.mult).then_inc(s_nf.h, 1)

        @blk.vector
        def _(dve):
            dve.memset(vs[:, :, :, :], 0.0).then_inc(s_init.h, 1)
            s_init.wait(dve, 1)
            dve.memset(vs[:, :, :, DK:DK + 1], 1.0).then_inc(s_init.h, 1)
            dve.memset(zs[KR:KR + NM, :, :], 1.0).then_inc(s_init.h, 1)
            dve.memset(ot[:, :, :], 1.0).then_inc(s_init.h, 1)
            dve.memset(ob[:, :, :], 0.0).then_inc(s_init.h, 1)
            dve.memset(mp_all[:, NM * NT:P], 0.0).then_inc(s_init.h, 1)
            if rel:
                dve.memset(skp[:, :, :, :], 0.0).then_inc(s_init.h, 1)
                dve.memset(delta[:, 0, 0, 0:64], 0.0).then_inc(s_init.h, 1)
                dve.memset(delta[:, 1, NT - 1, 64:P], 0.0).then_inc(s_init.h, 1)
            s_init.wait(dve, NINIT)
            for u in range(64):
                amax(dve, 0, 0, u)
            m_parts(dve, 0, 0)
            m_copy(dve, 0)
            for u in range(EARLY):
                amax(dve, 1, 1, u)
            with dve.Fori(0, HEADS // U) as it:
                for p in range(U):
                    t = U * it + p
                    for n in range(64):
                        if n == banks_until(F_STEP):
                            divide(dve, t, p, it + 1)
                        if n < 64 - EARLY:
                            amax(dve, t + 1, p + 1, EARLY + n)
                            continue
                        if n == 64 - EARLY:
                            m_parts(dve, t + 1, p + 1)
                        if n == 64 - EARLY + M_COPY:
                            m_copy(dve, t + 1)
                        amax(dve, t + 2, p + 2, n - (64 - EARLY))
            divide(dve, HEADS, 0, 0)
            s_nf.wait(dve, HEADS + 1)

        def copy_out(act, n, kind, release):
            s_fl.wait(act, n + 1)
            release()
            pos = ring_static(n)
            act.activation(pr[:, pos % NP, :], psS[:, pos % 2, :], ACT.Exp if kind == "E" else ACT.Copy
                           ).then_inc(s_cp.h, 1)

        def release_ring(eng, t, n):
            m = n - NP
            tt = t
            if m < 0:
                m, tt = m + NR, t - 1
            kind, c, _ = ring[m]
            if kind == "R":
                s_rw[c].wait(eng, 32 * (tt + 2 + 1))
            else:
                s_us.wait(eng, NUSE * tt + use_no[m] + 1)

        def window_exp(act, t, p, i):
            s_m.wait(act, MS * t + 2)
            act.activation(sw[:, p % 2, i, :], sw[:, p % 2, i, :], ACT.Exp, bias=nm[:, p % 2, i:i + 1]
                           ).then_inc(s_we.h, 1)

        def evacuate_o(act, t, p, c):
            s_us.wait(act, NUSE * t + use_no[chunk_end[c]] + 1)
            f_done(act, t - 1)
            act.activation(ot[:, p % 2, c * G:(c + 1) * G], psO[:, :], ACT.Copy).then_inc(s_oev.h, 1)

        @blk.scalar
        def _(act):
            s_init.wait(act, NINIT)
            if rel:
                for n in range(RPRO):
                    copy_out(act, n, "R", lambda: n >= NP and s_rw[n % 4].wait(act, 32 * (n // 4)))
                for c in range(4):
                    s_rw[c].wait(act, 64)
            for n in range(2):
                copy_out(act, At(0, n), ring[n][0], lambda: None)
            with act.Fori(0, HEADS // U) as it:
                for p in range(U):
                    t = U * it + p
                    for n in range(2, NR + 2):
                        k, m = n // NR, n % NR
                        if rel and n < 10:
                            for i in range(2 * n - 4, 2 * n - 2):
                                window_exp(act, t, p, i)
                        copy_out(act, At(t + k, m), ring[m][0], lambda: release_ring(act, t + k, m))
                        if n - 2 in chunk_end:
                            evacuate_o(act, t, p, chunk_end.index(n - 2))
            if rel:
                for n in range(2, 4):
                    copy_out(act, At(HEADS, n), "F", lambda: release_ring(act, HEADS, n))

        def a_unit(pe, t, p, u):
            i, k = u // 4, u % 4
            if u == 0:
                s_qz[p % U].wait(pe, 16 * NLD * ((t - p % U) // U + 1) if isinstance(t, int)
                                 else 16 * NLD * (t.it + p // U + 1))
            tv = t if isinstance(t, int) else t.value
            s_amax.wait(pe, 64 * tv + u - 1)
            z0 = (i * P if rel else 0) + k * G
            pe.matmul(psA[:, u % 2, :], qs[0:KR, p % U, i * P:(i + 1) * P], zs[0:KR, p % U, z0:z0 + G],
                      start=True, stop=True).then_inc(s_a.h, 1)

        class Head:
            def __init__(self, it, k):
                self.it, self.value = it, U * it + k

        def m_transpose(pe, tv):
            s_m.wait(pe, MS * (tv + 1))
            s_nf.wait(pe, tv)
            pe.transpose(psF[:, 0:4, :].rearrange("p a b -> p (a b)"), mp_all[:, :], ident[:, :]
                         ).then_inc(s_mt.h, 1)

        def fill(pe, n, kind, c, j, t, it, p):
            pos = ring_static(n)
            s_cp.wait(pe, n + (-1))
            dst = psS[:, pos % 2, :]
            if kind == "R":
                sl = (p + 2) % U
                if c == 0:
                    s_qz[sl].wait(pe, 16 * NLD * ((t + 2) // U + 1 if isinstance(t, int) else it + (p + 2) // U + 1))
                for i in range(4):
                    last = pe.matmul(dst[:, i * W:(i + 1) * W], qs[0:KR, sl, (4 * c + i) * P:(4 * c + i + 1) * P],
                                     e_stack[0:KR, :], start=True, stop=True)
                    if i == 1:
                        yield
            elif kind == "F":
                s_pr[c].wait(pe, 32 * t)
                for side in range(2):
                    for i in range(4):
                        last = pe.transpose(dst[:, side * G + i * P:side * G + (i + 1) * P],
                                            skp[:, side, 4 * c + i, :], ident[:, :])
                    if side == 0:
                        yield
            elif kind == "W":
                s_we.wait(pe, NT * t + 4 * c + 4)
                for side in range(2):
                    for i in range(4):
                        last = pe.transpose(dst[:, side * G + i * P:side * G + (i + 1) * P],
                                            sw[:, p % 2, 4 * c + i, (1 - side) * P:(2 - side) * P], ident[:, :])
                    if side == 0:
                        yield
            else:
                if c == 0 and j == 0:
                    s_mq.wait(pe, 16 * (t + 1))
                for e, bank in enumerate(banks(c, j)):
                    for z, lo, hi in bank:
                        last = pe.matmul(dst[:, e * G + lo:e * G + hi], zs[0:KR + NM, p % U, z * P:(z + 1) * P],
                                         qs[0:KR + NM, p % U, c * G + lo:c * G + hi], start=True, stop=True)
                    if e == 0:
                        yield
            last.then_inc(s_fl.h, 1)
            yield

        def use(pe, n, kind, c, j, t, p):
            pos = ring_static(n)
            if kind == "R":
                return
            s_cp.wait(pe, n + 1)
            src = pr[:, pos % NP, :]
            v = vs[:, p % 2, :, :]
            if kind == "F":
                if c == 0:
                    s_oev.wait(pe, 4 * t)
                    s_mr.wait(pe, t + 1)
                for i in range(4):
                    final(pe, p - 1, 4 * c + i, src)
                last = final_last[0]
            elif kind == "W":
                for side in range(2):
                    for i in range(4):
                        z = 4 * c + i + (0 if side == 1 else NROT)
                        last = pe.matmul(psO[32 * i:32 * i + 32, i * P:(i + 1) * P], v[:, z, :],
                                         src[:, side * G + i * P:side * G + (i + 1) * P],
                                         start=False, stop=side == 1, tile_position=(0, 32 * i),
                                         skip_group_check=True)
            else:
                if c == 0 and j == 0:
                    s_v.wait(pe, NV * (t + 1))
                if j == 0:
                    s_oev.wait(pe, 4 * t + c)
                nb = 14 if rel else 16
                for e, bank in enumerate(banks(c, j)):
                    m = 2 * j + e
                    for z, lo, hi in bank:
                        q = m % 4
                        last = pe.matmul(psO[32 * q:32 * q + 32, lo:hi], v[:, z, :], src[:, e * G + lo:e * G + hi],
                                         start=m < 4, stop=not rel and m >= nb - 4, tile_position=(0, 32 * q),
                                         skip_group_check=rel)
            last.then_inc(s_us.h, 1)

        final_last = [None]

        def final(pe, par, i, src):
            out = psF[:, i, :]
            final_last[0] = pe.matmul(out, ot[:, par % 2, i * P:(i + 1) * P], sel[:, :], start=True, stop=not rel)
            if rel:
                for side in range(2):
                    k = i % 4
                    final_last[0] = pe.matmul(out, src[:, side * G + k * P:side * G + (k + 1) * P], ev[:, side, :],
                                              start=False, stop=side == 1)

        def final_plain(pe, t, p):
            s_oev.wait(pe, 4 * t)
            s_mr.wait(pe, t + 1)
            for i in range(NT):
                final(pe, p - 1, i, None)
            final_last[0].then_inc(s_fm.h, 1)

        @blk.tensor
        def _(pe):
            s_init.wait(pe, NINIT)
            if rel:
                for n in range(RPRO):
                    for _ in fill(pe, n, "R", n % 4, 0, n // 4 - 2, None, n // 4 - 2):
                        pass
            for u in range(64):
                a_unit(pe, 0, 0, u)
            m_transpose(pe, 0)
            for u in range(EARLY):
                a_unit(pe, 1, 1, u)
            for n in range(2):
                for _ in fill(pe, At(0, n), *ring[n], 0, None, 0):
                    pass
            with pe.Fori(0, HEADS // U) as it:
                for p in range(U):
                    t = U * it + p
                    done = 0
                    for step in range(NSTEP):
                        stops = 0
                        new = banks_until(step) - done
                        for n in (2 * step + 2, 2 * step + 3):
                            k, n = n // NR, n % NR
                            for _ in fill(pe, At(t + k, n), *ring[n], t + k, it, p + k):
                                stops += 1
                                while done < banks_until(step) - new + (1, 1, 2, new)[stops - 1]:
                                    ahead = 1 if done < 64 - EARLY else 2
                                    a_unit(pe, Head(it, p + ahead), p + ahead, (EARLY + done) % 64)
                                    done += 1
                        assert stops == 4
                        for n in (2 * step, 2 * step + 1):
                            use(pe, At(t, n), *ring[n], t, p)
                        if not rel and step == F_STEP - 1:
                            final_plain(pe, t, p)
                        if step == M_STEP:
                            m_transpose(pe, t + 1)
            if rel:
                for n in range(4):
                    if n >= 2:
                        for _ in fill(pe, At(HEADS, n), *ring[n], HEADS, None, 0):
                            pass
                    use(pe, At(HEADS, n), *ring[n], HEADS, 0)
            else:
                final_plain(pe, HEADS, 0)
def selection(nc, ident, sel):
    with ExitStack() as ctx:
        s_sel, = sems = [ctx.enter_context(nc.semaphore(n)) for n in ("s_sel",)]
        ctx.callback(clear_semaphores, nc, sems)
        blk = ctx.enter_context(nc.Block())
        @blk.vector
        def _(dve):
            dve.reduce_sum(sel[:, :], ident[:, :].rearrange("p (j c) -> p c j", c=32), AX.X).then_inc(s_sel, 1)
            dve.wait_ge(s_sel, 1)


def rel_tables(nc, emb_k, emb_v, e_stack, ev, ev_side, k_side, dr_r, dr_p):
    with ExitStack() as ctx:
        def sb(name, shape, dt=F32):
            return ctx.enter_context(nc.sbuf_tensor("rt_" + name, shape, dt))

        ekt = sb("ekt", [DK, 2 * MRP + 1])
        diff = sb("diff", [DK, W])
        rest = sb("rest", [DK, W])
        parts = sb("parts", [DK, 3, W], BF16)
        evr = sb("evr", [P, DK])
        zero = sb("zero", [P, 16 * W])
        s_ld, s_z, s_zd, s_e, s_st = sems = [ctx.enter_context(nc.semaphore("rt_" + n)) for n in
                                             ("s_ld", "s_z", "s_zd", "s_e", "s_st")]
        ctx.callback(clear_semaphores, nc, sems)
        blk = ctx.enter_context(nc.Block())

        @blk.scalar
        def _(act):
            act.wait_ge(s_z, 1)
            for tab in (dr_r, dr_p):
                for par in range(2):
                    for side in range(2):
                        act.dma_start(tab[par, side].rearrange("i q r -> q i r"),
                                      zero[:, :].rearrange("p (i r) -> p i r", r=W)).then_inc(s_zd, 16)
            act.wait_ge(s_zd, 16 * 8)

        @blk.sync
        def _(sp):
            with nc.allow_non_contiguous_dma(reason="129 x 16 elements, once"):
                sp.dma_start(ekt[:, :], emb_k.rearrange("r d -> d r")).then_inc(s_ld, 16)
            sp.dma_start(evr[:, :], emb_v[0:P, :]).then_inc(s_ld, 16)
            for side, r in ((0, 0), (1, 2 * MRP)):
                row = emb_v[r:r + 1, :]
                sp.dma_start(ev_side[:, side, :, :], bass.AP(row.tensor, row.offset, [[0, P], [0, NROT], [1, DK]])
                             ).then_inc(s_ld, 16)
                for hh in range(P // DK):
                    sp.dma_start(k_side[hh * DK:(hh + 1) * DK, side:side + 1],
                                 emb_k[r:r + 1, :].rearrange("r d -> d r")).then_inc(s_ld, 16)
            sp.wait_ge(s_e, 9)
            for i, part in enumerate(K_PART):
                sp.dma_start(e_stack[i * DK:(i + 1) * DK, :], parts[:, part, :]).then_inc(s_st, 16)
            sp.wait_ge(s_st, 16 * len(K_PART))

        @blk.vector
        def _(dve):
            dve.memset(zero[:, :], 0.0).then_inc(s_z, 1)
            dve.memset(ev[:, :, :], 0.0).then_inc(s_e, 1)
            dve.wait_ge(s_ld, 16 * (4 + 2 * P // DK))
            dve.wait_ge(s_e, 1)
            dve.tensor_scalar(diff[:, 0:P], ekt[:, 0:P], ekt[:, 0:1], None, ALU.subtract).then_inc(s_e, 1)
            dve.tensor_scalar(diff[:, P:W], ekt[:, 0:P], ekt[:, P:P + 1], None, ALU.subtract).then_inc(s_e, 1)
            for side in range(2):
                dve.tensor_tensor(out=ev[:, side, 0:DK], in0=evr[:, :], in1=ev_side[:, side, 0, :],
                                  op=ALU.subtract).then_inc(s_e, 1)
            dve.wait_ge(s_e, 5)
            dve.tensor_copy(parts[:, 0, :], diff[:, :]).then_inc(s_e, 1)
            dve.wait_ge(s_e, 6)
            dve.tensor_tensor(out=rest[:, :], in0=diff[:, :], in1=parts[:, 0, :], op=ALU.subtract).then_inc(s_e, 1)
            dve.wait_ge(s_e, 7)
            dve.tensor_copy(parts[:, 1, :], rest[:, :]).then_inc(s_e, 1)
            dve.wait_ge(s_e, 8)
            dve.tensor_tensor(out=parts[:, 2, :], in0=rest[:, :], in1=parts[:, 1, :], op=ALU.subtract).then_inc(s_e, 1)
            dve.wait_ge(s_e, 9)


def load_small(nc, name, pairs, adds=()):
    with ExitStack() as ctx:
        s_ld, s_add = sems = [ctx.enter_context(nc.semaphore(n)) for n in (name + "_ld", name + "_add")]
        ctx.callback(clear_semaphores, nc, sems)
        blk = ctx.enter_context(nc.Block())
        @blk.sync
        def _(sp):
            with nc.allow_non_contiguous_dma(reason="small vectors, once"):
                for dst, src in pairs:
                    sp.dma_start(dst, src).then_inc(s_ld, 16)
            sp.wait_ge(s_ld, 16 * len(pairs))

        @blk.vector
        def _(dve):
            if adds:
                dve.wait_ge(s_ld, 16 * len(pairs))
                for out, a, b in adds:
                    dve.tensor_tensor(out=out, in0=a, in1=b, op=ALU.add).then_inc(s_add, 1)
                dve.wait_ge(s_add, len(adds))


def out_stage(nc, tag, o_rows, wo, bo, resid, dst, ident):
    with ExitStack() as ctx:
        def sb(name, shape, dt=F32):
            return ctx.enter_context(nc.sbuf_tensor(f"{tag}_{name}", shape, dt))

        sems = []

        def sem(name, credit=32):
            sems.append(Sem(ctx, nc, f"{tag}_{name}", credit))
            return sems[-1]

        res = sb("res", [P, 2, TPG, D])
        rb = sb("rb", [P, 2, TPG, D])
        y = sb("y", [P, 2, TPG, D])
        ot = sb("ot", [P, 2, CH, G])
        os = sb("os", [P, 2, TPG, D])
        psT = ctx.enter_context(nc.psum_tensor(f"{tag}_psT", [P, CH, G], F32))
        psY = ctx.enter_context(nc.psum_tensor(f"{tag}_psY", [P, 2, 2, D], F32))
        s_ld = [sem(f"s_ld{i}") for i in range(2)]
        s_st = [sem(f"s_st{i}") for i in range(2)]
        s_os = [sem(f"s_os{i}") for i in range(2)]
        s_rb, s_t, s_ot, s_y, s_yo = (sem(n) for n in ("s_rb", "s_t", "s_ot", "s_y", "s_yo"))
        ctx.callback(clear_semaphores, nc, sems)
        blk = ctx.enter_context(nc.Block())
        rv = resid.rearrange("(g j p) c -> g p j c", p=P, j=TPG)
        ov = o_rows.rearrange("(g j p) c -> g p j c", p=P, j=TPG)
        dv = dst.rearrange("(g j p) c -> g p j c", p=P, j=TPG)

        @blk.sync
        def _(sp):
            give_credits(sp, sems)
            with sp.Fori(0, NG // 2) as it:
                for q in range(2):
                    g = 2 * it + q
                    wait_all(sp, (s_rb, g - 1),
                             (s_t, CH * (g - 1)))
                    sp.dma_start(os[:, q, :, :], ov[bass.ds(g, 1), :, :, :].rearrange("g p j c -> p (g j) c")
                                 ).then_inc(s_os[q].h, 16)
                    sp.dma_start(res[:, q, :, :], rv[bass.ds(g, 1), :, :, :].rearrange("g p j c -> p (g j) c")
                                 ).then_inc(s_ld[q].h, 16)

        @blk.gpsimd
        def _(pool):
            with pool.Fori(0, NG // 2) as it:
                for q in range(2):
                    g = 2 * it + q
                    s_ld[q].wait(pool, 16 * (it + 1))
                    s_yo.wait(pool, 2 * (g - 1))
                    pool.tensor_tensor(out=rb[:, q, :, :], in0=res[:, q, :, :],
                                       in1=bo[:, :].rearrange("p (a c) -> p a c", a=1).to_broadcast([P, TPG, D]),
                                       op=ALU.add).then_inc(s_rb.h, 1)

        @blk.tensor
        def _(pe):
            with pe.Fori(0, NG // 2) as it:
                for q in range(2):
                    g = 2 * it + q
                    s_os[q].wait(pe, 16 * (it + 1))
                    for c in range(CH):
                        s_ot.wait(pe, CH * (g - 1) + c + 1)
                        for j in range(TPG):
                            last = pe.transpose(psT[:, c, j * P:(j + 1) * P],
                                                os[:, q, j, c * P:(c + 1) * P], ident[:, :])
                        last.then_inc(s_t.h, 1)
                    s_ot.wait(pe, CH * (g + 1))
                    for v in range(2):
                        s_yo.wait(pe, 2 * (g - 1) + v + 1)
                        for i in range(2):
                            for c in range(CH):
                                j = 2 * v + i
                                last = pe.matmul(psY[:, v, i, :], ot[:, q, c, j * P:(j + 1) * P], wo[:, c, :],
                                                 start=c == 0, stop=c == CH - 1)
                        last.then_inc(s_y.h, 1)

        @blk.scalar
        def _(act):
            with act.Fori(0, NG // 2) as it:
                for q in range(2):
                    g = 2 * it + q
                    for c in range(CH):
                        s_t.wait(act, CH * g + c + 1)
                        if c == 0:
                            s_y.wait(act, 2 * (g - 1))
                        act.activation(ot[:, q, c, :], psT[:, c, :], ACT.Copy).then_inc(s_ot.h, 1)
                    s_yo.wait(act, 2 * (g + 1))
                    act.dma_start(dv[bass.ds(g, 1), :, :, :].rearrange("g p j c -> p (g j) c"), y[:, q, :, :]
                                  ).then_inc(s_st[q].h, 16)
            for q in range(2):
                s_st[q].wait(act, 16 * NG // 2)

        @blk.vector
        def _(dve):
            with dve.Fori(0, NG // 2) as it:
                for q in range(2):
                    g = 2 * it + q
                    s_rb.wait(dve, g + 1)
                    s_st[q].wait(dve, 16 * it)
                    for v in range(2):
                        s_y.wait(dve, 2 * g + v + 1)
                        dve.tensor_tensor(out=y[:, q, 2 * v:2 * v + 2, :], in0=psY[:, v, :, :],
                                          in1=rb[:, q, 2 * v:2 * v + 2, :], op=ALU.add).then_inc(s_yo.h, 1)


def routing(nc, lg, gb, ew, ew_t, b1_dram, b1_t, ident):
    TT = T // P
    with ExitStack() as ctx:
        def sb(name, shape, dt=F32):
            return ctx.enter_context(nc.sbuf_tensor("ro_" + name, shape, dt))

        top = sb("top", [P, TT, 8])
        idx = sb("idx", [P, TT, 8], mybir.dt.uint32)
        idf = sb("idf", [P, TT, 2])
        number = sb("number", [P, NE])
        dif, ex, den, w = sb("dif", [P, TT]), sb("ex", [P, TT]), sb("den", [P, TT]), sb("w", [P, TT, 2])
        hot = sb("hot", [P, 2, TT, NE])
        b1r = sb("b1r", [NE * FC, P])
        psE = ctx.enter_context(nc.psum_tensor("ro_psE", [P, TT * P], F32))
        s_n, s_lg, s_top, s_i, s_v, s_ex, s_b, s_t, s_o = sems = [ctx.enter_context(nc.semaphore("ro_" + n)) for n in
            ("s_n", "s_lg", "s_top", "s_i", "s_v", "s_ex", "s_b", "s_t", "s_o")]
        ctx.callback(clear_semaphores, nc, sems)
        blk = ctx.enter_context(nc.Block())

        @blk.sync
        def _(sp):
            sp.dma_start(b1r[:, :], b1_dram.rearrange("e (f p) -> (e f) p", p=P)).then_inc(s_b, 16)

        @blk.gpsimd
        def _(pool):
            for e in range(NE):
                pool.memset(number[:, e:e + 1], float(e)).then_inc(s_n, 1)

        @blk.scalar
        def _(act):
            act.wait_ge(s_v, 2)
            act.activation(ex[:, :], dif[:, :], ACT.Exp).then_inc(s_ex, 1)

        @blk.vector
        def _(dve):
            dve.tensor_tensor(out=lg[:, :, :], in0=lg[:, :, :],
                              in1=gb[:, :].rearrange("p (a e) -> p a e", a=1).to_broadcast([P, TT, NE]),
                              op=ALU.add).then_inc(s_lg, 1)
            dve.wait_ge(s_lg, 1)
            for j in range(TT):
                dve.max(out=top[:, j, :], in_=lg[:, j, :]).then_inc(s_top, 1)
            for j in range(TT):
                dve.wait_ge(s_top, j + 1)
                dve.max_index(idx[:, j, :], top[:, j, :], lg[:, j, :]).then_inc(s_i, 1)
            dve.wait_ge(s_i, TT)
            n = [0]

            def then(ins, wait=True):
                n[0] += 1
                ins.then_inc(s_v, 1)
                if wait:
                    dve.wait_ge(s_v, n[0])

            then(dve.tensor_copy(idf[:, :, :], idx[:, :, 0:2]))
            then(dve.tensor_tensor(out=dif[:, :], in0=top[:, :, 1], in1=top[:, :, 0], op=ALU.subtract))
            dve.wait_ge(s_ex, 1)
            then(dve.tensor_scalar_add(den[:, :], ex[:, :], 1.0))
            then(dve.reciprocal(w[:, :, 0], den[:, :]))
            then(dve.tensor_tensor(out=w[:, :, 1], in0=ex[:, :], in1=w[:, :, 0], op=ALU.mult))
            dve.wait_ge(s_n, NE)
            for k in range(2):
                then(dve.tensor_tensor(out=hot[:, k, :, :], in0=number[:, :].rearrange("p (a e) -> p a e", a=1
                                       ).to_broadcast([P, TT, NE]),
                                       in1=idf[:, :, k:k + 1].to_broadcast([P, TT, NE]), op=ALU.is_equal))
                then(dve.tensor_tensor(out=hot[:, k, :, :], in0=hot[:, k, :, :],
                                       in1=w[:, :, k:k + 1].to_broadcast([P, TT, NE]), op=ALU.mult))
            then(dve.tensor_tensor(out=ew[:, :, :], in0=hot[:, 0, :, :], in1=hot[:, 1, :, :], op=ALU.add))
            dve.wait_ge(s_t, 1)
            dve.tensor_copy(b1_t[:, :], psE[:, 0:NE * FC]).then_inc(s_o, 1)
            dve.wait_ge(s_t, 2)
            dve.tensor_copy(ew_t[:, :], psE[0:NE, :]).then_inc(s_o, 1)
            dve.wait_ge(s_o, 2)

        @blk.tensor
        def _(pe):
            pe.wait_ge(s_b, 16)
            pe.transpose(psE[:, 0:NE * FC], b1r[:, :], ident[0:NE * FC, 0:NE * FC]).then_inc(s_t, 1)
            pe.wait_ge(s_v, 10)
            pe.wait_ge(s_o, 1)
            for j in range(TT):
                last = pe.transpose(psE[0:NE, j * P:(j + 1) * P], ew[:, j, :], ident[:, :])
            last.then_inc(s_t, 1)


def moe_stage(nc, hT, ew, ew_t, w1, b1_t, w2, b2_sb, x1, f2, out, ident):
    TT = T // P
    with ExitStack() as ctx:
        def sb(name, shape, dt=F32):
            return ctx.enter_context(nc.sbuf_tensor("mo_" + name, shape, dt))

        sems = []

        def sem(name, credit=256):
            sems.append(Sem(ctx, nc, "mo_" + name, credit))
            return sems[-1]

        acc = sb("acc", [P, TT, D])
        w1s = sb("w1s", [P, 2, CH, DFF])
        w2s = sb("w2s", [P, 2, FC, D])
        hid = sb("hid", [P, 2, FC, G])
        b1_now = sb("b1_now", [P, 2, FC])
        a_in = sb("a_in", [P, 2, TPG, D])
        b_in = sb("b_in", [P, 2, TPG, D])
        psH = ctx.enter_context(nc.psum_tensor("mo_psH", [P, 4, G], F32))
        psY = ctx.enter_context(nc.psum_tensor("mo_psY", [P, 4, G], F32))
        s_w = [sem(f"s_w{i}") for i in range(2)]
        s_in = [sem(f"s_in{i}") for i in range(2)]
        s_h, s_r, s_y, s_acc, s_xf, s_0, s_b = (sem(n) for n in ("s_h", "s_r", "s_y", "s_acc", "s_xf", "s_0", "s_b"))
        s_out, s_b1 = sem("s_out"), sem("s_b1")
        ctx.callback(clear_semaphores, nc, sems)
        blk = ctx.enter_context(nc.Block())

        def load_w(sp, e, q, it):
            s_y.wait(sp, TT * (2 * (it - 1) + q + 1))
            sp.dma_start(w1s[:, q, :, :], w1[bass.ds(e, 1), :, :].rearrange("e (c p) f -> p (e c) f", p=P)
                         ).then_inc(s_w[q].h, 16)
            sp.dma_start(w2s[:, q, :, :], w2[bass.ds(e, 1), :, :].rearrange("e (f p) d -> p (e f) d", p=P)
                         ).then_inc(s_w[q].h, 16)

        @blk.sync
        def _(sp):
            give_credits(sp, sems)
            xv = x1.rearrange("(g j p) c -> g p j c", p=P, j=TPG)
            fv = f2.rearrange("(g j p) c -> g p j c", p=P, j=TPG)
            for g in range(NG):
                s_xf.wait(sp, g - 1)
                sp.dma_start(a_in[:, g % 2, :, :], xv[g]).then_inc(s_in[g % 2].h, 16)
                sp.dma_start(b_in[:, g % 2, :, :], fv[g]).then_inc(s_in[g % 2].h, 16)
                if g == 1:
                    for q in range(2):
                        load_w(sp, q, q, 0)
            with sp.Fori(0, NE // 2 - 1) as it:
                for q in range(2):
                    load_w(sp, 2 * (it + 1) + q, q, it + 1)
            s_acc.wait(sp, TT * NE)
            sp.dma_start(out.rearrange("(j p) c -> p j c", p=P), acc[:, :, :]).then_inc(s_out.h, 16)
            s_out.wait(sp, 16)

        @blk.tensor
        def _(pe):
            for j in range(TT):
                s_b.wait(pe, j - 3)
                pe.matmul(psY[:, j % 4, 0:D], ew_t[:, j * P:(j + 1) * P], b2_sb[:, :], start=True, stop=True
                          ).then_inc(s_0.h, 1)
            with pe.Fori(0, NE // 2) as it:
                for q in range(2):
                    with pe.Fori(0, NG // 2) as gg:
                        for r in range(2):
                            s_w[q].wait(pe, 32 * (it + 1))
                            e = 2 * it + q
                            g = 2 * gg + r
                            n = e * NG + g
                            for f in range(FC):
                                s_r.wait(pe, FC * n + f - 3)
                                for c in range(CH):
                                    last = pe.matmul(psH[:, f % 4, :], w1s[:, q, c, f * P:(f + 1) * P],
                                                     hT[:, c, bass.ds(g * G, G)], start=c == 0, stop=c == CH - 1)
                                last.then_inc(s_h.h, 1)
                            for j in range(TPG):
                                s_acc.wait(pe, TPG * n + j - 3)
                                if j == 0:
                                    s_b.wait(pe, TT)
                                for f in range(FC):
                                    if j == 0:
                                        s_r.wait(pe, FC * n + f + 1)
                                    last = pe.matmul(psY[:, j, 0:D], hid[:, r, f, j * P:(j + 1) * P],
                                                     w2s[:, q, f, :], start=f == 0, stop=f == FC - 1)
                                last.then_inc(s_y.h, 1)

        @blk.scalar
        def _(act):
            with act.Fori(0, NE // 2) as it:
                for q in range(2):
                    with act.Fori(0, NG // 2) as gg:
                        for r in range(2):
                            e = 2 * it + q
                            n = e * NG + 2 * gg + r
                            s_y.wait(act, TPG * (n - 1))
                            s_b1.wait(act, e + 1)
                            for f in range(FC):
                                s_h.wait(act, FC * n + f + 1)
                                act.activation(hid[:, r, f, :], psH[:, f % 4, :], ACT.Relu,
                                               bias=b1_now[:, q, f:f + 1]).then_inc(s_r.h, 1)

        @blk.gpsimd
        def _(pool):
            for g in range(NG):
                s_in[g % 2].wait(pool, 32 * (g // 2 + 1))
                pool.tensor_tensor(out=acc[:, g * TPG:(g + 1) * TPG, :], in0=a_in[:, g % 2, :, :],
                                   in1=b_in[:, g % 2, :, :], op=ALU.add).then_inc(s_xf.h, 1)

        @blk.vector
        def _(dve):
            for j in range(TT):
                s_xf.wait(dve, j // TPG + 1)
                s_0.wait(dve, j + 1)
                dve.tensor_tensor(out=acc[:, j, :], in0=psY[:, j % 4, 0:D], in1=acc[:, j, :], op=ALU.add
                                  ).then_inc(s_b.h, 1)
            s_b.wait(dve, TT)
            with dve.Fori(0, NE // 2) as it:
                for q in range(2):
                    s_r.wait(dve, FC * NG * (2 * it + q - 1))
                    dve.tensor_copy(b1_now[:, q, :], b1_t[:, bass.ds((2 * it + q) * FC, FC)]).then_inc(s_b1.h, 1)
                    with dve.Fori(0, NG // 2) as gg:
                        for r in range(2):
                            e = 2 * it + q
                            g = 2 * gg + r
                            n = e * NG + g
                            s_acc.wait(dve, TPG * (n - (NG - 1)))
                            for j in range(TPG):
                                s_y.wait(dve, TPG * n + j + 1)
                                row = acc[:, bass.ds(g * TPG + j, 1), :].rearrange("p a c -> p (a c)")
                                dve.scalar_tensor_tensor(
                                    out=row, in0=psY[:, j, 0:D],
                                    scalar=ew[:, bass.ds(g * TPG + j, 1), bass.ds(e, 1)].rearrange("p a e -> p (a e)"),
                                    in1=row, op0=ALU.mult, op1=ALU.add).then_inc(s_acc.h, 1)


def program(nc, A, out):
    def dram(name, shape, dt=F32):
        return nc.dram_tensor(name, shape, dt).ap()

    q_parts, kl_parts, kr_parts = (dram(n, (3, D, T), BF16) for n in ("q_parts", "kl_parts", "kr_parts"))
    v_rows, o_rows, x1, f_rows, f2_rows = (dram(n, (T, D)) for n in
                                           ("v_rows", "o_rows", "x1_rows", "f_rows", "f2_rows"))
    dr_r, dr_p = (dram(n, (2, 2, NT, P, W)) for n in ("rel_logits", "rel_probs"))

    def column(vec, c):
        return vec[c * P:(c + 1) * P].rearrange("(p a) -> p a", a=1)

    with ExitStack() as top:
        def sb(stack, name, shape, dt=F32):
            return stack.enter_context(nc.sbuf_tensor(name, shape, dt))

        ident = sb(top, "ident", [P, P])
        sel = sb(top, "sel", [P, 32])
        ident_and_ones(nc, ident)
        selection(nc, ident, sel)

        with ExitStack() as one:
            e_stack = sb(one, "e_stack", [P, W], BF16)
            ev = sb(one, "ev", [P, 2, 32])
            ev_side = sb(one, "ev_side", [P, 2, NROT, DK])
            with ExitStack() as st:
                k_side = sb(st, "k_side", [P, 2])
                wt = sb(st, "w_qkv_t", [P, CH, 3 * D])
                cols = sb(st, "cols", [P, 8])
                vb = sb(st, "v_bias", [P, D])
                rel_tables(nc, A["attn_embK"], A["attn_embV"], e_stack, ev, ev_side, k_side, dr_r, dr_p)
                load_small(nc, "l1", [(vb[:, :], bcast_rows(A["attn_bv"]))]
                           + [(cols[:, c:c + 1], column(A["attn_bq"], c)) for c in range(CH)]
                           + [(cols[:, 2 + c:3 + c], column(A["attn_bk"], c)) for c in range(CH)],
                           [(cols[:, 4 + 2 * s + c:5 + 2 * s + c], cols[:, 2 + c:3 + c], k_side[:, s:s + 1])
                            for s in range(2) for c in range(CH)])
                for i, n in enumerate(("Wq", "Wk", "Wv")):
                    transposed_weight(nc, n + "T", A["attn_" + n], wt[:, :, i * D:(i + 1) * D], ident)
                units = [(c * P, cols[:, c:c + 1], 1.0, (q_parts, c * P)) for c in range(CH)]
                for s, dst in ((0, kl_parts), (1, kr_parts)):
                    units += [(D + c * P, cols[:, 4 + 2 * s + c:5 + 2 * s + c], 1.0, (dst, c * P)) for c in range(CH)]
                ln_proj_stage(nc, "rel", A["attn_x"], ident, wt, units, vb, {"v": v_rows})
            attention_stage(nc, True, ident, sel, q_parts, (kl_parts, kr_parts), v_rows, o_rows,
                            {"e_stack": e_stack, "ev": ev, "ev_side": ev_side, "dr_r": dr_r, "dr_p": dr_p})
            wo = sb(one, "wo_t", [P, CH, D])
            bo = sb(one, "bo", [P, D])
            load_small(nc, "o1", [(bo[:, :], bcast_rows(A["attn_bo"]))])
            transposed_weight(nc, "WoT", A["attn_Wo"], wo, ident)
            out_stage(nc, "o1", o_rows, wo, bo, A["attn_x"], x1, ident)

        with ExitStack() as two:
            with ExitStack() as st:
                wt = sb(st, "w_qkv", [P, CH, 3 * D])
                cols = sb(st, "cols2", [P, 8])
                gain = sb(st, "gain1", [P, 2, CH])
                vb = sb(st, "v_bias2", [P, D])
                load_small(nc, "l2", [(wt[:, :, :], A["ffn_w_qkv"].rearrange("(c p) n -> p c n", p=P)),
                                      (vb[:, :], bcast_rows(A["ffn_b_qkv"][2 * D:3 * D]))]
                           + [(cols[:, c:c + 1], column(A["ffn_b_qkv"], c)) for c in range(2 * CH)]
                           + [(gain[:, k, c:c + 1], column(A[n], c)) for c in range(CH)
                              for k, n in enumerate(("ffn_ln1_g", "ffn_ln1_b"))])
                units = [(c * P, cols[:, c:c + 1], float(DK) ** -0.5, (q_parts, c * P)) for c in range(CH)]
                units += [(D + c * P, cols[:, 2 + c:3 + c], 1.0, (kl_parts, c * P)) for c in range(CH)]
                ln_proj_stage(nc, "plain", x1, ident, wt, units, vb, {"v": v_rows}, gain=gain, save_ln=f_rows)
            attention_stage(nc, False, ident, sel, q_parts, (kl_parts, None), v_rows, o_rows)
            wo = sb(two, "wo2", [P, CH, D])
            bo = sb(two, "bo2", [P, D])
            load_small(nc, "o2", [(bo[:, :], bcast_rows(A["ffn_b_o"])),
                                  (wo[:, :, :], A["ffn_w_o"].rearrange("(c p) n -> p c n", p=P))])
            out_stage(nc, "o2", o_rows, wo, bo, f_rows, f2_rows, ident)

        with ExitStack() as three:
            hT = sb(three, "hT_all", [P, CH, T])
            lg = sb(three, "gate_logits", [P, T // P, NE])
            ew = sb(three, "ew", [P, T // P, NE])
            ew_t = sb(three, "ew_t", [NE, T])
            b1_t = sb(three, "b1_t", [P, NE * FC])
            b2_sb = sb(three, "b2_sb", [NE, D])
            with ExitStack() as st:
                gate = sb(st, "gate", [P, CH, NE])
                gain = sb(st, "gain2", [P, 2, CH])
                gb = sb(st, "gate_bias", [P, NE])
                load_small(nc, "l3", [(gate[:, :, :], A["ffn_gate_w"].rearrange("(c p) e -> p c e", p=P)),
                                      (gb[:, :], bcast_rows(A["ffn_gate_b"])), (b2_sb[:, :], A["ffn_b2"])]
                           + [(gain[:, k, c:c + 1], column(A[n], c)) for c in range(CH)
                              for k, n in enumerate(("ffn_ln2_g", "ffn_ln2_b"))])
                ln_proj_stage(nc, "gate", f2_rows, ident, None, [], None,
                              {"hT_all": hT, "gate": gate, "logits": lg}, gain=gain)
                routing(nc, lg, gb, ew, ew_t, A["ffn_b1"], b1_t, ident)
            moe_stage(nc, hT, ew, ew_t, A["ffn_W1"], b1_t, A["ffn_W2"], b2_sb, x1, f2_rows, out, ident)


def kernel(**inputs):
    import numpy as _np
    import concourse.bacc as _bacc
    from concourse import mybir as _mybir
    from concourse.bass_utils import run_bass_kernel_spmd as _run

    nc = _bacc.Bacc("TRN2", target_bir_lowering=False, num_devices=1)
    arrays, args = {}, {}
    for name, value in inputs.items():
        if name == "L0_attn_mask":
            continue
        a = _np.ascontiguousarray(value)
        if name == "L0_attn_x":
            a = a.reshape(T, D)
        short = name[3:]
        arrays[short] = a
        args[short] = nc.dram_tensor(short, a.shape, _mybir.dt.from_np(a.dtype), kind="ExternalInput").ap()
    out = nc.dram_tensor("out", (T, D), _mybir.dt.float32, kind="ExternalOutput").ap()
    program(nc, args, out)
    r = _run(nc, [arrays], core_ids=[0])
    return r.results[0]["out"].reshape(NB, S, D)
```

```python
import numpy as np
import concourse.bass as bass
import concourse.mybir as mybir
from contextlib import ExitStack

F32 = mybir.dt.float32
BF16 = mybir.dt.bfloat16
ACT = mybir.ActivationFunctionType
ALU = mybir.AluOpType
AX = mybir.AxisListType

P = 128
D = 256
CH = D // P
NH = 16
DK = D // NH
NB = 2
S = 2048
T = NB * S
NT = S // P
MRP = 64
NE = 8
DFF = 4 * D
FC = DFF // P
G = 512
TPG = G // P
NG = T // G
EPS = 1e-5
Q_PART = (0, 0, 0, 1, 1, 2)
K_PART = (0, 1, 2, 0, 1, 0)
KR = len(Q_PART) * DK
NM = 3


def ready(engine, value):
    return value if isinstance(value, int) else engine.snap(value)


def bcast_rows(ap, n=P):
    return bass.AP(ap.tensor, ap.offset, [[0, n]] + [list(x) for x in ap.ap])


class Sem:

    def __init__(self, ctx, nc, name, credit):
        self.h = ctx.enter_context(nc.semaphore(name))
        self.credit = credit

    def wait(self, engine, n):
        if not isinstance(n, int) or n > 0:
            engine.wait_ge(self.h, n + self.credit)


def wait_all(engine, *waits):
    waits = [(s, n if isinstance(n, int) else engine.to_reg(n + s.credit)) for s, n in waits]
    for s, n in waits:
        if not isinstance(n, int):
            engine.wait_ge(s.h, n)
        elif n > 0:
            engine.wait_ge(s.h, n + s.credit)


def clear_semaphores(nc, sems):
    with nc.Block() as blk:
        @blk.sync
        def _(sp):
            for s in sems:
                sp.sem_clear(s.h if isinstance(s, Sem) else s)


def give_credits(engine, sems):
    for s in sems:
        engine.sem_inc(s.h, s.credit)


def ident_and_ones(nc, ident):
    with ExitStack() as ctx:
        s_zero, s_ident = sems = [ctx.enter_context(nc.semaphore(n)) for n in ("s_zero", "s_ident")]
        ctx.callback(clear_semaphores, nc, sems)
        blk = ctx.enter_context(nc.Block())
        @blk.gpsimd
        def _(pool):
            pool.memset(ident[:, :], 0.0).then_inc(s_zero, 1)
            pool.wait_ge(s_zero, 1)
            pool.affine_select(out=ident[:, :], in_=ident[:, :], compare_op=ALU.not_equal, fill=1.0,
                               base=0, pattern=[[-1, P]], channel_multiplier=1).then_inc(s_ident, 1)
            pool.wait_ge(s_ident, 1)


def transposed_weight(nc, name, w_dram, out_sb, ident):
    with ExitStack() as ctx:
        raw = ctx.enter_context(nc.sbuf_tensor(name + "_raw", [P, CH, D], F32))
        ps = ctx.enter_context(nc.psum_tensor(name + "_ps", [P, CH, D], F32))
        s_load, s_tr, s_out = sems = [ctx.enter_context(nc.semaphore(name + n)) for n in ("_load", "_tr", "_out")]
        ctx.callback(clear_semaphores, nc, sems)
        blk = ctx.enter_context(nc.Block())

        @blk.sync
        def _(sp):
            sp.dma_start(raw[:, :, :], w_dram.rearrange("(a p) c -> p a c", p=P)).then_inc(s_load, 16)

        @blk.tensor
        def _(pe):
            pe.wait_ge(s_load, 16)
            for a in range(CH):
                for c in range(CH):
                    last = pe.transpose(ps[:, c, a * P:(a + 1) * P], raw[:, a, c * P:(c + 1) * P], ident[:, :])
            last.then_inc(s_tr, 1)

        @blk.vector
        def _(dve):
            dve.wait_ge(s_tr, 1)
            dve.tensor_copy(out_sb[:, :, :], ps[:, :, :]).then_inc(s_out, 1)
            dve.wait_ge(s_out, 1)


def ln_proj_stage(nc, mode, src, ident, weights, cols, v_bias, dram, gain=None, save_ln=None,
                  zero_fill=None):
    two_ln = save_ln is not None
    NS = 2 if two_ln else 1
    attn = mode != "gate"
    units = cols if attn else []
    NU = len(units)
    with ExitStack() as ctx:
        def sb(name, shape, dt=F32):
            return ctx.enter_context(nc.sbuf_tensor(f"{mode}_{name}", shape, dt))

        def ps(name, shape):
            return ctx.enter_context(nc.psum_tensor(f"{mode}_{name}", shape, F32))

        sems = []

        def sem(name, credit=16):
            sems.append(Sem(ctx, nc, f"{mode}_{name}", credit))
            return sems[-1]

        x = sb("x", [P, 2, TPG, D])
        h = sb("h", [P, 2, NS, TPG, D])
        stats = sb("stats", [P, 2, NS, TPG, 6])
        moments = sb("moments", [P, 2, NS, 5, TPG])
        mean = sb("mean", [P, 2, NS, TPG])
        ve = sb("ve", [P, 2, NS, TPG])
        sd = sb("sd", [P, 2, NS, TPG])
        rs = sb("rs", [P, 2, NS, TPG])
        hT = sb("hT", [P, 2, CH, G])
        full, r1, r2 = (sb(n, [P, 2, G]) for n in ("full", "r1", "r2")) if attn else (None, None, None)
        parts = sb("parts", [P, 4, 3, G], BF16) if attn else None
        vout = sb("vout", [P, 2, TPG, D]) if attn else None
        psT = ps("psT", [P, CH, G])
        psU = ps("psU", [P, 2, G])
        psV = ps("psV", [P, 2, 2, D])
        s_x = [sem(f"s_x{i}") for i in range(2)]
        s_stat, s_sum, s_mean, s_var, s_ve, s_sd, s_rs, s_h = (sem(n) for n in
            ("s_stat", "s_sum", "s_mean", "s_var", "s_ve", "s_sd", "s_rs", "s_h"))
        s_f = [sem(f"s_f{i}") for i in range(2)]
        s_t, s_hT, s_u, s_full, s_hi, s_r1, s_mid, s_lo, s_v, s_vo = (sem(n) for n in
            ("s_t", "s_hT", "s_u", "s_full", "s_hi", "s_r1", "s_mid", "s_lo", "s_v", "s_vo"))
        s_po = [sem(f"s_po{i}") for i in range(4)]
        s_vd = [sem(f"s_vd{i}") for i in range(2)]
        s_zero = sem("s_zero")
        if not attn:
            hT_all, gate = dram["hT_all"], dram["gate"]
            lg, s_lg, s_all = dram["logits"], sem("s_lg"), sem("s_all")
        ctx.callback(clear_semaphores, nc, sems)
        blk = ctx.enter_context(nc.Block())

        def slot(q, m):
            return (NU * q + m) % 4

        def stored(it, q, m):
            return NU * 2 // 4 * it + (NU * q + m) // 4

        src_v = src.rearrange("(g j p) c -> g p j c", p=P, j=TPG)

        @blk.sync
        def _(sp):
            give_credits(sp, sems)
            with sp.Fori(0, NG // 2) as it:
                for q in range(2):
                    g = 2 * it + q
                    s_h.wait(sp, NS * TPG * (2 * it + q - 1))
                    sp.dma_start(x[:, q, :, :], src_v[bass.ds(g, 1), :, :, :].rearrange("g p j c -> p (g j) c")
                                 ).then_inc(s_x[q].h, 16)
                    if zero_fill:
                        zero, tables = zero_fill
                        sp.dma_start(tables[bass.ds(g, 1), :, :, :].rearrange("g i q r -> q (g i) r"),
                                     zero[:, :].rearrange("p (i r) -> p i r", r=W)).then_inc(s_zero.h, 16)
            s_h.wait(sp, NS * TPG * (NG - 1))
            sp.dma_start(x[:, 0, :, :], src_v[0]).then_inc(s_x[0].h, 16)
            s_x[0].wait(sp, 16 * (NG // 2 + 1))
            s_x[1].wait(sp, 16 * NG // 2)
            if zero_fill:
                s_zero.wait(sp, 16 * NG)

        def normalise(dve, g, it, q):
            s_x[q].wait(dve, 16 * (it + 1))
            for n in range(NS):
                k = TPG * (NS * g + n)
                data = x[:, q] if n == 0 else h[:, q, 0]
                for j in range(TPG):
                    dve.bn_stats(stats[:, q, n, j, :], data[:, j, :]).then_inc(s_stat.h, 1)
                yield
                st, mo = stats[:, q, n, :, :], moments[:, q, n, :, :]
                s_stat.wait(dve, k + TPG)
                for o, a, b, op in ((0, 1, 4, ALU.add), (1, 1, 4, ALU.subtract), (2, 2, 5, ALU.add)):
                    dve.tensor_tensor(out=mo[:, o, :], in0=st[:, :, a], in1=st[:, :, b], op=op
                                      ).then_inc(s_sum.h, 1)
                yield
                s_sum.wait(dve, 3 * (NS * g + n + 1))
                dve.tensor_scalar(mean[:, q, n, :], mo[:, 0, :], 0.5, None, ALU.mult).then_inc(s_mean.h, 1)
                dve.scalar_tensor_tensor(out=mo[:, 3, :], in0=mo[:, 1, :], scalar=0.25, in1=mo[:, 1, :],
                                         op0=ALU.mult, op1=ALU.mult).then_inc(s_mean.h, 1)
                yield
                s_mean.wait(dve, 2 * (NS * g + n + 1))
                dve.scalar_tensor_tensor(out=mo[:, 4, :], in0=mo[:, 2, :], scalar=1.0 / D, in1=mo[:, 3, :],
                                         op0=ALU.mult, op1=ALU.add).then_inc(s_var.h, 1)
                yield
                s_var.wait(dve, NS * g + n + 1)
                dve.tensor_scalar_add(ve[:, q, n, :], mo[:, 4, :], EPS).then_inc(s_ve.h, 1)
                yield
                s_sd.wait(dve, NS * g + n + 1)
                dve.reciprocal(rs[:, q, n, :], sd[:, q, n, :]).then_inc(s_rs.h, 1)
                yield
                s_rs.wait(dve, NS * g + n + 1)
                if n == 0 and two_ln:
                    s_f[q].wait(dve, 16 * it)
                if n == NS - 1:
                    s_t.wait(dve, CH * (g - 1))
                for j in range(TPG):
                    dve.tensor_scalar(h[:, q, n, j, :], data[:, j, :], mean[:, q, n, j:j + 1],
                                      rs[:, q, n, j:j + 1], ALU.subtract, ALU.mult).then_inc(s_h.h, 1)
                if n < NS - 1:
                    s_h.wait(dve, k + TPG)
                yield

        LN_STEPS, VE_STEP = 7 * NS, 4
        PER = -(-LN_STEPS // (NU + 2)) if NU else LN_STEPS

        def roots(act, g, q, after):
            for n in range(NS):
                if after is None or (7 * n + VE_STEP) // PER == after:
                    s_ve.wait(act, NS * g + n + 1)
                    act.activation(sd[:, q, n, :], ve[:, q, n, :], ACT.Sqrt).then_inc(s_sd.h, 1)

        @blk.vector
        def _(dve):
            for _ in normalise(dve, 0, 0, 0):
                pass
            with dve.Fori(0, NG // 2) as it:
                for q in range(2):
                    g = 2 * it + q
                    ahead = normalise(dve, g + 1, it + q, 1 - q)
                    for step in range(NU + 2 if NU else 0):
                        if step < NU:
                            m, n, w = step, NU * g + step, step % 2
                            _, bias, scale, _ = units[m]
                            s_u.wait(dve, n + 1)
                            s_hi.wait(dve, n - 1)
                            s_r1.wait(dve, n - 1)
                            dve.tensor_scalar(full[:, w, :], psU[:, w, :], bias, scale, ALU.add, ALU.mult
                                              ).then_inc(s_full.h, 1)
                        if 0 <= step - 1 < NU:
                            m, n, w = step - 1, NU * g + step - 1, (step - 1) % 2
                            s_full.wait(dve, n + 1)
                            s_hi.wait(dve, n + 1)
                            s_mid.wait(dve, n - 1)
                            s_lo.wait(dve, n - 1)
                            dve.tensor_tensor(out=r1[:, w, :], in0=full[:, w, :], in1=parts[:, slot(q, m), 0, :],
                                              op=ALU.subtract).then_inc(s_r1.h, 1)
                        if 0 <= step - 2 < NU:
                            m, n, w = step - 2, NU * g + step - 2, step % 2
                            s_mid.wait(dve, n + 1)
                            s_po[slot(q, m)].wait(dve, 16 * stored(it, q, m))
                            dve.tensor_tensor(out=parts[:, slot(q, m), 2, :], in0=r1[:, w, :],
                                              in1=parts[:, slot(q, m), 1, :], op=ALU.subtract).then_inc(s_lo.h, 1)
                        for _, _ in zip(range(PER), ahead):
                            pass
                    if not NU:
                        for _ in ahead:
                            pass
                    if attn:
                        for v in range(2):
                            s_v.wait(dve, 2 * g + v + 1)
                            if v == 0:
                                s_vd[q].wait(dve, 16 * it)
                            dve.tensor_tensor(out=vout[:, q, 2 * v:2 * v + 2, :], in0=psV[:, v, :, :],
                                              in1=v_bias[:, :].rearrange("p (a c) -> p a c", a=1).to_broadcast([P, 2, D]),
                                              op=ALU.add).then_inc(s_vo.h, 1)
                    else:
                        s_hT.wait(dve, CH * (g + 1))
                        dve.tensor_copy(hT_all[:, :, bass.ds(g * G, G)], hT[:, q, :, :]).then_inc(s_all.h, 1)
                        s_lg.wait(dve, g + 1)
                        dve.tensor_copy(lg[:, bass.ds(g * TPG, TPG), :], psU[:, 0, 0:TPG * NE].rearrange(
                            "p (j e) -> p j e", e=NE)).then_inc(s_vo.h, 1)
            s_vo.wait(dve, (2 if attn else 1) * NG)

        @blk.scalar
        def _(act):
            if two_ln:
                save_v = save_ln.rearrange("(g j p) c -> g p j c", p=P, j=TPG)
            if attn:
                v_v = dram["v"].rearrange("(g j p) c -> g p j c", p=P, j=TPG)
            roots(act, 0, 0, None)
            with act.Fori(0, NG // 2) as it:
                for q in range(2):
                    g = 2 * it + q
                    if two_ln:
                        s_h.wait(act, NS * TPG * g + TPG)
                        act.dma_start(save_v[bass.ds(g, 1), :, :, :].rearrange("g p j c -> p (g j) c"),
                                      h[:, q, 0, :, :]).then_inc(s_f[q].h, 16)
                    for c in range(CH):
                        s_t.wait(act, CH * g + c + 1)
                        if c == 0 and attn:
                            s_v.wait(act, 2 * (g - 1))
                        if c == 0 and not attn:
                            s_lg.wait(act, g - 1)
                            s_all.wait(act, g - 1)
                        dst = hT[:, q, c, :]
                        if gain is None:
                            act.activation(dst, psT[:, c, :], ACT.Copy).then_inc(s_hT.h, 1)
                        else:
                            act.activation(dst, psT[:, c, :], ACT.Identity, bias=gain[:, 1, c:c + 1],
                                           scale=gain[:, 0, c:c + 1]).then_inc(s_hT.h, 1)
                    if not NU:
                        roots(act, g + 1, 1 - q, None)
                    for step in range(NU + 2 if NU else 0):
                        if step < NU:
                            m, n = step, NU * g + step
                            s_full.wait(act, n + 1)
                            s_po[slot(q, m)].wait(act, 16 * stored(it, q, m))
                            act.activation(parts[:, slot(q, m), 0, :], full[:, m % 2, :], ACT.Copy
                                           ).then_inc(s_hi.h, 1)
                        if 0 <= step - 1 < NU:
                            m, n = step - 1, NU * g + step - 1
                            s_r1.wait(act, n + 1)
                            act.activation(parts[:, slot(q, m), 1, :], r1[:, m % 2, :], ACT.Copy
                                           ).then_inc(s_mid.h, 1)
                        if 0 <= step - 2 < NU:
                            m, n = step - 2, NU * g + step - 2
                            dst, row = units[m][3]
                            s_hi.wait(act, n + 1)
                            s_mid.wait(act, n + 1)
                            s_lo.wait(act, n + 1)
                            act.dma_start(dst[:, row:row + P, bass.ds(g * G, G)].rearrange("a p t -> p a t"),
                                          parts[:, slot(q, m), :, :]).then_inc(s_po[slot(q, m)].h, 16)
                        roots(act, g + 1, 1 - q, step)
                    if attn:
                        s_vo.wait(act, 2 * g + 2)
                        act.dma_start(v_v[bass.ds(g, 1), :, :, :].rearrange("g p j c -> p (g j) c"),
                                      vout[:, q, :, :]).then_inc(s_vd[q].h, 16)
            for q in range(2):
                if two_ln:
                    s_f[q].wait(act, 16 * NG // 2)
                if attn:
                    s_vd[q].wait(act, 16 * NG // 2)
            if attn:
                for w in range(4):
                    s_po[w].wait(act, 16 * NU * NG // 4)

        @blk.tensor
        def _(pe):
            with pe.Fori(0, NG // 2) as it:
                for q in range(2):
                    g = 2 * it + q
                    s_h.wait(pe, TPG * NS * (g + 1))
                    for c in range(CH):
                        s_hT.wait(pe, CH * (g - 1) + c + 1)
                        for j in range(TPG):
                            last = pe.transpose(psT[:, c, j * P:(j + 1) * P],
                                                h[:, q, NS - 1, j, c * P:(c + 1) * P], ident[:, :])
                        last.then_inc(s_t.h, 1)
                    s_hT.wait(pe, CH * (g + 1))
                    for m, (col, _, _, _) in enumerate(units):
                        n = NU * g + m
                        s_full.wait(pe, n - 1)
                        for c in range(CH):
                            last = pe.matmul(psU[:, m % 2, :], weights[:, c, col:col + P], hT[:, q, c, :],
                                             start=c == 0, stop=c == CH - 1)
                        last.then_inc(s_u.h, 1)
                    if attn:
                        for v in range(2):
                            s_vo.wait(pe, 2 * (g - 1) + v + 1)
                            for i in range(2):
                                for c in range(CH):
                                    j = 2 * v + i
                                    last = pe.matmul(psV[:, v, i, :], hT[:, q, c, j * P:(j + 1) * P],
                                                     weights[:, c, 2 * D:3 * D], start=c == 0, stop=c == CH - 1)
                            last.then_inc(s_v.h, 1)
                    else:
                        s_vo.wait(pe, g)
                        for j in range(TPG):
                            for c in range(CH):
                                last = pe.matmul(psU[:, 0, j * NE:(j + 1) * NE], hT[:, q, c, j * P:(j + 1) * P],
                                                 gate[:, c, :], start=c == 0, stop=c == CH - 1)
                        last.then_inc(s_lg.h, 1)
U = 4
HEADS = NB * NH
NROT = 15
NZ = 2 * NROT + 1
W = 2 * P


def attention_stage(nc, rel, ident, sel, qd, kd, vd, o_rows, rel_tabs=None):
    tag = "ra" if rel else "pa"
    nz = NZ if rel else NT
    zw = nz * P
    exp_scale = 1.0
    lead = 3
    ring = []
    if rel:
        ring += [("F", c, 0) for c in range(4)]
    for c in range(4):
        ring += [("E", c, j) for j in range(7 if rel else 8)]
        if rel:
            ring += [("W", c, 0)]
            if c % 2:
                ring += [("R", c - 1, 0), ("R", c, 0)]
    NR = len(ring)
    RPRO = 8 if rel else 0
    used = [k != "R" for k, _, _ in ring]
    use_no = [sum(used[:n]) for n in range(NR)]
    NUSE = sum(used)
    NP = 4
    place = {(k, c): n for n, (k, c, _) in enumerate(ring)}
    chunk_end = [place["W" if rel else "E", c] for c in range(4)]

    NSTEP = NR // 2
    EARLY = 64 * 5 // NSTEP

    def banks_until(step):
        return 64 * (step + 1) // NSTEP

    M_STEP = next(n for n in range(NSTEP) if banks_until(n) >= 64 - EARLY) + 1
    M_COPY = banks_until(M_STEP) - (64 - EARLY)
    A_AT = (1, 2, 2, 2, 8)
    FINALS = (2, 3, 4, 5)

    def banks(c, j):
        if not rel:
            return [[(2 * j + e, 0, G)] for e in range(2)]
        every = [[(4 * c + 4 + z, 0, G)] for z in range(11)]
        every += [[(4 * c + 1 + z, 0, P * (z + 1)), (4 * c + 15 + z, P * (z + 1), G)] for z in range(3)]
        return every[2 * j:2 * j + 2]

    with ExitStack() as ctx:
        def sb(name, shape, dt=F32):
            return ctx.enter_context(nc.sbuf_tensor(f"{tag}_{name}", shape, dt))

        def ps(name, shape):
            return ctx.enter_context(nc.psum_tensor(f"{tag}_{name}", shape, F32))

        sems = []

        def sem(name, credit=64):
            sems.append(Sem(ctx, nc, f"{tag}_{name}", credit))
            return sems[-1]

        qs = sb("qs", [P, U, S], BF16)
        zs = sb("zs", [P, U, zw], BF16)
        vall = sb("vall", [P, NB, NT, D])
        vs = sb("vs", [P, 2, nz, 32])
        pr = sb("p", [P, NP, 2 * G])
        ot = sb("ot", [P, 2, S])
        pm = sb("pm", [P, 2, NT, 5])
        nm = sb("nm", [P, 2, NT])
        mhi = sb("mhi", [P, NT], BF16)
        mmid = sb("mmid", [P, NT], BF16)
        mres = sb("mres", [P, NT])
        mp_all = sb("mp", [P, P])
        mp = mp_all[:, 0:NM * NT].rearrange("p (m i) -> p m i", i=NT)
        mrow = sb("mrow", [NM * NT, P], BF16)
        rec = sb("rec", [P, NT])
        ob = sb("ob", [P, NT, U * DK])
        if rel:
            e_stack, ev, ev_side = rel_tabs["e_stack"], rel_tabs["ev"], rel_tabs["ev_side"]
            dr_r, dr_p = rel_tabs["dr_r"], rel_tabs["dr_p"]
            delta = sb("delta", [P, 2, NT, P])
            sw = sb("sw", [P, 2, NT, W])
            vraw = sb("vraw", [P, NT, DK])
            skp = sb("skp", [P, 2, NT, P])
        psS = ps("psS", [P, 2, 2 * G])
        psA = ps("psA", [P, 2, G])
        psO = ps("psO", [P, G])
        psF = ps("psF", [P, NT, 32])

        s_init = sem("s_init")
        s_qz = [sem(f"s_qz{i}") for i in range(U)]
        s_vall = sem("s_vall")
        s_v = sem("s_v")
        s_a, s_amax = sem("s_a"), sem("s_amax")
        s_m, s_mt, s_mr, s_mq = sem("s_m"), sem("s_mt"), sem("s_mr"), sem("s_mq")
        s_fl, s_cp, s_us = sem("s_fl"), sem("s_cp"), sem("s_us")
        s_ob = sem("s_ob")
        s_oev, s_fm, s_rec, s_nf = sem("s_oev"), sem("s_fm"), sem("s_rec"), sem("s_nf")
        if rel:
            s_sw, s_wm = sem("s_sw"), sem("s_wm")
            s_fa = sem("s_fa")
            s_we = sem("s_we")
            s_pw = [sem(f"s_pw{c}") for c in range(4)]
            s_pr = [sem(f"s_pr{c}") for c in range(4)]
            s_rw = [sem(f"s_rw{c}") for c in range(4)]
            s_dr = [sem(f"s_dr{c}") for c in range(4)]
        ctx.callback(clear_semaphores, nc, sems)
        blk = ctx.enter_context(nc.Block())

        def head(t):
            n = t % HEADS
            return n // NH, n % NH

        NLD = 2 * 6 if not rel else 18

        def load_stacks(sp, t, p):
            b, h = head(t)
            slot = p % U
            row = ready(sp, h * DK)
            col = {lo: ready(sp, b * S + lo) for lo in ((0, 64) if rel else (0,))}
            s_us.wait(sp, NUSE * (t - 3))
            n = 0
            for part_of, dst, srcs in ((Q_PART, qs, [(qd, 0, S, 0)]),
                                       (K_PART, zs, [(kd[1], 64, S, 0), (kd[0], 0, S - 64, S - 64)] if rel
                                        else [(kd[0], 0, S, 0)])):
                for src, lo, hi, at in srcs:
                    for i, part in enumerate(part_of):
                        sp.dma_start(dst[i * DK:(i + 1) * DK, slot, at:at + hi - lo],
                                     src[part, bass.ds(row, DK), bass.ds(col[lo], hi - lo)]
                                     ).then_inc(s_qz[slot].h, 16)
                        n += 1
            assert n == NLD

        def skew(tab, t_par, side, i0, n, k0, k1):
            base = ((t_par * 2 + side) * NT + i0) * P * W + P + k0
            return bass.AP(tab.tensor, tab.offset + base, [[W - 1, P], [P * W, n], [1, k1 - k0]])

        def rows(tab, t_par, side, i0, n):
            base = ((t_par * 2 + side) * NT + i0) * P * W + (P if side == 0 else 0)
            return bass.AP(tab.tensor, tab.offset + base, [[W, P], [P * W, n], [1, P]])

        def window_pieces(c):
            i0 = 4 * c
            left = [(0, 0, 1, 64, P), (0, 1, 3, 0, P)] if c == 0 else [(0, i0, 4, 0, P)]
            right = [(1, i0, 3, 0, P), (1, NT - 1, 1, 0, 64)] if c == 3 else [(1, i0, 4, 0, P)]
            return left + right

        def write_p(sp, t, p):
            for c in range(4):
                wait_all(sp, (s_we, NT * t + 4 * c + 4),
                         (s_pr[c], 32 * (t - 1)))
                for side, i0, n, k0, k1 in window_pieces(c):
                    col = P if side == 0 else 0
                    sp.dma_start(skew(dr_p, p % 2, side, i0, n, k0, k1),
                                 sw[:, p % 2, i0:i0 + n, col + k0:col + k1]).then_inc(s_pw[c].h, 16)

        def read_p(sp, t, p):
            for c in range(4):
                np_ = len(window_pieces(c))
                wait_all(sp, (s_pw[c], 16 * np_ * (t + 1)),
                         (s_fl, RPRO + NR * t + c + 1))
                for side in range(2):
                    sp.dma_start(skp[:, side, 4 * c:4 * c + 4, :], rows(dr_p, p % 2, side, 4 * c, 4)
                                 ).then_inc(s_pr[c].h, 16)

        def trip_r(sp, t, p, c, n):
            src = pr[:, RING_P(n), :].rearrange("p (i s r) -> p i s r", i=4, s=2)
            wait_all(sp, (s_cp, n + 1),
                     (s_dr[c], DR(c) * (t - 1)))
            for side in range(2):
                sp.dma_start(rows(dr_r, p % 2, side, 4 * c, 4), src[:, :, side, :]).then_inc(s_rw[c].h, 16)
            wait_all(sp, (s_rw[c], 32 * (t + 1)),
                     (s_amax, 64 * (t - 1) + 16 * (c + 1)))
            for side, i0, m, k0, k1 in window_pieces(c):
                sp.dma_start(delta[:, side, i0:i0 + m, k0:k1], skew(dr_r, p % 2, side, i0, m, k0, k1)
                             ).then_inc(s_dr[c].h, 16)

        def DR(c):
            return 16 * len(window_pieces(c))

        def RING_P(n):
            return ring_static(n) % NP

        def ring_static(n):
            return n if isinstance(n, int) else n.position

        class At:
            def __init__(self, t, n):
                self.value = RPRO + NR * t + n
                self.position = RPRO + n

            def __add__(self, k):
                return self.value + k

        assert NR % NP == 0 and RPRO % NP == 0

        def send_m(sp, t, p):
            s_mr.wait(sp, t + 1)
            sp.dma_start(qs[KR:KR + NM, p % U, :], mrow[:, :]).then_inc(s_mq.h, 16)

        def store_o(sp, t):
            b, h = head(t + HEADS - U)
            row, col = ready(sp, b * S), ready(sp, h * DK)
            s_nf.wait(sp, t + 1)
            sp.dma_start(o_rows[bass.ds(row, S), bass.ds(col, U * DK)].rearrange("(i q) c -> q i c", q=P),
                         ob[:, :, :]).then_inc(s_ob.h, 16)

        @blk.sync
        def _(sp):
            give_credits(sp, sems)
            for b in range(NB):
                if rel:
                    sp.dma_start(vall[:, b, 0:NROT, :], vd[b * S + 64:b * S + 64 + NROT * P, :].rearrange(
                        "(z p) c -> p z c", p=P)).then_inc(s_vall.h, 16)
                    sp.dma_start(vall[0:64, b, NROT, :], vd[(b + 1) * S - 64:(b + 1) * S, :]).then_inc(s_vall.h, 16)
                    sp.dma_start(vall[64:P, b, NROT, :], vd[b * S:b * S + 64, :]).then_inc(s_vall.h, 16)
                else:
                    sp.dma_start(vall[:, b, :, :], vd[b * S:(b + 1) * S, :].rearrange(
                        "(z p) c -> p z c", p=P)).then_inc(s_vall.h, 16)
            for t in range(lead):
                load_stacks(sp, t, t)
            if rel:
                for t in range(2):
                    for c in range(4):
                        trip_r(sp, t, t, c, 4 * t + c)
            send_m(sp, 0, 0)
            with sp.Fori(0, HEADS // U) as it:
                for p in range(U):
                    t = U * it + p
                    if rel:
                        write_p(sp, t, p)
                    load_stacks(sp, t + lead, p + lead)
                    if rel:
                        read_p(sp, t, p)
                        for c in range(2):
                            trip_r(sp, t + 2, p + 2, c, At(t, place["R", c]))
                    if p == 0:
                        store_o(sp, t)
                    send_m(sp, t + 1, p + 1)
                    if rel:
                        for c in range(2, 4):
                            trip_r(sp, t + 2, p + 2, c, At(t, place["R", c]))
            for t in range(HEADS, HEADS + lead):
                s_qz[t % U].wait(sp, 16 * NLD * (t // U + 1))
            s_mq.wait(sp, 16 * (HEADS + 1))
            store_o(sp, HEADS)
            s_ob.wait(sp, 16 * (HEADS // U + 1))
            if rel:
                for c in range(4):
                    s_dr[c].wait(sp, DR(c) * (HEADS + 2))
                    s_pr[c].wait(sp, 32 * HEADS)

        NV = 5 if rel else 1
        NINIT = 9 if rel else 6

        def lay_v(pool, t, p):
            b, h = head(t)
            b, col = ready(pool, b), ready(pool, h * DK)
            s_us.wait(pool, NUSE * (t - 1))
            if not rel:
                pool.tensor_copy(vs[:, p % 2, :, 0:DK], vall[:, bass.ds(b, 1), :, bass.ds(col, DK)].rearrange(
                    "p b z d -> p (b z) d")).then_inc(s_v.h, 1)
                return
            s_v.wait(pool, NV * t)
            pool.tensor_copy(vraw[:, :, :], vall[:, bass.ds(b, 1), :, bass.ds(col, DK)].rearrange(
                "p b z d -> p (b z) d")).then_inc(s_v.h, 1)
            k = 1
            for side, z0 in ((1, 0), (0, NROT + 1)):
                s_v.wait(pool, NV * t + k)
                pool.tensor_tensor(out=vs[:, p % 2, z0:z0 + NROT, 0:DK],
                                   in0=vraw[:, 0:NROT, :],
                                   in1=ev_side[:, side, 0:NROT, :], op=ALU.add).then_inc(s_v.h, 1)
                k += 1
            for side, lo in ((1, 0), (0, 64)):
                s_v.wait(pool, NV * t + k)
                pool.tensor_tensor(out=vs[lo:lo + 64, p % 2, NROT, 0:DK],
                                   in0=vraw[lo:lo + 64, NROT, :],
                                   in1=ev_side[lo:lo + 64, side, 0, :], op=ALU.add).then_inc(s_v.h, 1)
                k += 1


        @blk.gpsimd
        def _(pool):
            s_vall.wait(pool, 16 * NB * (3 if rel else 1))
            s_init.wait(pool, NINIT)
            lay_v(pool, 0, 0)
            with pool.Fori(0, HEADS // U) as it:
                for p in range(U):
                    lay_v(pool, U * it + p + 1, p + 1)


        def amax(dve, t, p, u):
            i, k = u // 4, u % 4
            bank = psA[:, u % 2, :]
            if rel and k == 1 and i > 0:
                window_max(dve, t, p, i - 1)
            s_a.wait(dve, 64 * t + u + 1)
            lo, hi = 0, G
            if rel and k == 0:
                s_dr[i // 4].wait(dve, DR(i // 4) * (t + 1))
                if i % 4 == 0:
                    c = i // 4
                    s_we.wait(dve, NT * (t - 2) + 4 * c + 4)
                    s_pw[c].wait(dve, DR(c) * (t - 1))
                    s_us.wait(dve, NUSE * (t - 2) + use_no[chunk_end[c]] + 1)
            if rel and k in (0, 3):
                side = 1 if k == 0 else 0
                at = 0 if k == 0 else G - P
                col = P if side == 0 else 0
                lo, hi = (P, G) if k == 0 else (0, G - P)
                dve.tensor_tensor(out=sw[:, p % 2, i, col:col + P], in0=bank[:, at:at + P],
                                  in1=delta[:, side, i, :], op=ALU.add).then_inc(s_sw.h, 1)
            dve.reduce_max(pm[:, p % 2, i, k:k + 1], bank[:, lo:hi], AX.X).then_inc(s_amax.h, 1)

        def f_done(eng, t):
            s_fm.wait(eng, t + 1)

        def window_max(dve, t, p, i):
            s_sw.wait(dve, 2 * NT * t + 2 * i + 2)
            dve.reduce_max(pm[:, p % 2, i, 4:5], sw[:, p % 2, i, :], AX.X).then_inc(s_wm.h, 1)

        MS = 8

        def m_parts(dve, t, p):
            q = p % 2
            if rel:
                window_max(dve, t, p, NT - 1)
                s_wm.wait(dve, NT * (t + 1))
            s_amax.wait(dve, 64 * (t + 1))
            step = [0]

            def then(ins):
                step[0] += 1
                ins.then_inc(s_m.h, 1)
                if step[0] < MS:
                    s_m.wait(dve, MS * t + step[0])

            if rel:
                s_we.wait(dve, NT * (t - 1))
            s_mt.wait(dve, t)
            then(dve.reduce_max(mres[:, :], pm[:, q, :, 0:5 if rel else 4], AX.X))
            then(dve.tensor_scalar(nm[:, q, :], mres[:, :], -1.0, None, ALU.mult))
            then(dve.tensor_copy(mhi[:, :], nm[:, q, :]))
            then(dve.tensor_copy(mp[:, 0, :], mhi[:, :]))
            then(dve.tensor_tensor(out=mres[:, :], in0=nm[:, q, :], in1=mp[:, 0, :], op=ALU.subtract))
            then(dve.tensor_copy(mmid[:, :], mres[:, :]))
            then(dve.tensor_copy(mp[:, 1, :], mmid[:, :]))
            then(dve.tensor_tensor(out=mp[:, 2, :], in0=mres[:, :], in1=mp[:, 1, :], op=ALU.subtract))

        def m_copy(dve, t):
            s_mt.wait(dve, t + 1)
            s_mq.wait(dve, 16 * t)
            dve.tensor_copy(mrow[:, :], psF[0:NM * NT, 0:4, :].rearrange("p a b -> p (a b)")).then_inc(s_mr.h, 1)

        def add_rel_v(dve, t, p, c):
            s_us.wait(dve, NUSE * t + c + 1)
            half = slice(64 * (c % 2), 64 * (c % 2) + 64)
            dst = ot[half, (p - 1) % 2, c * G:(c + 1) * G]
            dve.tensor_tensor(out=dst, in0=psO[half, :], in1=dst, op=ALU.add).then_inc(s_fa.h, 1)

        def divide(dve, t, p, stores_before):
            col = (p - 1) % U * DK
            if col == 0:
                s_ob.wait(dve, 16 * stores_before)
            f_done(dve, t)
            s_nf.wait(dve, t)
            dve.reciprocal(rec[:, :], psF[:, :, DK]).then_inc(s_rec.h, 1)
            s_rec.wait(dve, t + 1)
            dve.tensor_tensor(out=ob[:, :, col:col + DK], in0=psF[:, :, 0:DK],
                              in1=rec[:, :].rearrange("p (i a) -> p i a", a=1).to_broadcast([P, NT, DK]),
                              op=ALU.mult).then_inc(s_nf.h, 1)

        @blk.vector
        def _(dve):
            dve.memset(vs[:, :, :, :], 0.0).then_inc(s_init.h, 1)
            s_init.wait(dve, 1)
            dve.memset(vs[:, :, :, DK:DK + 1], 1.0).then_inc(s_init.h, 1)
            dve.memset(zs[KR:KR + NM, :, :], 1.0).then_inc(s_init.h, 1)
            dve.memset(ot[:, :, :], 1.0).then_inc(s_init.h, 1)
            dve.memset(ob[:, :, :], 0.0).then_inc(s_init.h, 1)
            dve.memset(mp_all[:, NM * NT:P], 0.0).then_inc(s_init.h, 1)
            if rel:
                dve.memset(skp[:, :, :, :], 0.0).then_inc(s_init.h, 1)
                dve.memset(delta[:, 0, 0, 0:64], 0.0).then_inc(s_init.h, 1)
                dve.memset(delta[:, 1, NT - 1, 64:P], 0.0).then_inc(s_init.h, 1)
            s_init.wait(dve, NINIT)
            for u in range(64):
                amax(dve, 0, 0, u)
            m_parts(dve, 0, 0)
            m_copy(dve, 0)
            for u in range(EARLY):
                amax(dve, 1, 1, u)
            with dve.Fori(0, HEADS // U) as it:
                for p in range(U):
                    t = U * it + p
                    for n in range(64):
                        for step in range(2):
                            if rel and n == banks_until(step):
                                add_rel_v(dve, t, p, 2 * step)
                                add_rel_v(dve, t, p, 2 * step + 1)
                        if n == banks_until(FINALS[-1]):
                            divide(dve, t, p, it + 1)
                        if n < 64 - EARLY:
                            amax(dve, t + 1, p + 1, EARLY + n)
                            continue
                        if n == 64 - EARLY:
                            m_parts(dve, t + 1, p + 1)
                        if n == 64 - EARLY + M_COPY:
                            m_copy(dve, t + 1)
                        amax(dve, t + 2, p + 2, n - (64 - EARLY))
            if rel:
                for c in range(4):
                    add_rel_v(dve, HEADS, 0, c)
            divide(dve, HEADS, 0, 0)
            s_nf.wait(dve, HEADS + 1)

        def copy_out(act, n, kind, release):
            s_fl.wait(act, n + 1)
            release()
            pos = ring_static(n)
            act.activation(pr[:, pos % NP, :], psS[:, pos % 2, :], ACT.Exp if kind == "E" else ACT.Copy
                           ).then_inc(s_cp.h, 1)

        def release_ring(eng, t, n):
            m = n - NP
            tt = t
            if m < 0:
                m, tt = m + NR, t - 1
            kind, c, _ = ring[m]
            if kind == "R":
                s_rw[c].wait(eng, 32 * (tt + 2 + 1))
            else:
                s_us.wait(eng, NUSE * tt + use_no[m] + 1)

        def window_exp(act, t, p, i):
            s_m.wait(act, MS * t + 2)
            act.activation(sw[:, p % 2, i, :], sw[:, p % 2, i, :], ACT.Exp, bias=nm[:, p % 2, i:i + 1]
                           ).then_inc(s_we.h, 1)

        def evacuate_o(act, t, p, c):
            s_us.wait(act, NUSE * t + use_no[chunk_end[c]] + 1)
            f_done(act, t - 1)
            act.activation(ot[:, p % 2, c * G:(c + 1) * G], psO[:, :], ACT.Copy).then_inc(s_oev.h, 1)

        @blk.scalar
        def _(act):
            s_init.wait(act, NINIT)
            if rel:
                for n in range(RPRO):
                    copy_out(act, n, "R", lambda: n >= NP and s_rw[n % 4].wait(act, 32 * (n // 4)))
                for c in range(4):
                    s_rw[c].wait(act, 64)
            for n in range(2):
                copy_out(act, At(0, n), ring[n][0], lambda: None)
            with act.Fori(0, HEADS // U) as it:
                for p in range(U):
                    t = U * it + p
                    for n in range(2, NR + 2):
                        k, m = n // NR, n % NR
                        if rel and n < 10:
                            for i in range(2 * n - 4, 2 * n - 2):
                                window_exp(act, t, p, i)
                        copy_out(act, At(t + k, m), ring[m][0], lambda: release_ring(act, t + k, m))
                        if n - 2 in chunk_end:
                            evacuate_o(act, t, p, chunk_end.index(n - 2))
            if rel:
                for n in range(2, 4):
                    copy_out(act, At(HEADS, n), "F", lambda: release_ring(act, HEADS, n))

        def a_unit(pe, t, p, u):
            i, k = u // 4, u % 4
            if u == 0:
                s_qz[p % U].wait(pe, 16 * NLD * ((t - p % U) // U + 1) if isinstance(t, int)
                                 else 16 * NLD * (t.it + p // U + 1))
            tv = t if isinstance(t, int) else t.value
            s_amax.wait(pe, 64 * tv + u - 1)
            z0 = (i * P if rel else 0) + k * G
            pe.matmul(psA[:, u % 2, :], qs[0:KR, p % U, i * P:(i + 1) * P], zs[0:KR, p % U, z0:z0 + G],
                      start=True, stop=True).then_inc(s_a.h, 1)

        class Head:
            def __init__(self, it, k):
                self.it, self.value = it, U * it + k

        def m_transpose(pe, tv):
            s_m.wait(pe, MS * (tv + 1))
            s_nf.wait(pe, tv)
            pe.transpose(psF[:, 0:4, :].rearrange("p a b -> p (a b)"), mp_all[:, :], ident[:, :]
                         ).then_inc(s_mt.h, 1)

        def fill(pe, n, kind, c, j, t, it, p):
            pos = ring_static(n)
            s_cp.wait(pe, n + (-1))
            dst = psS[:, pos % 2, :]
            if kind == "R":
                sl = (p + 2) % U
                if c == 0:
                    s_qz[sl].wait(pe, 16 * NLD * ((t + 2) // U + 1 if isinstance(t, int) else it + (p + 2) // U + 1))
                for i in range(4):
                    last = pe.matmul(dst[:, i * W:(i + 1) * W], qs[0:KR, sl, (4 * c + i) * P:(4 * c + i + 1) * P],
                                     e_stack[0:KR, :], start=True, stop=True)
                    if i == 1:
                        yield
            elif kind == "F":
                s_pr[c].wait(pe, 32 * t)
                for side in range(2):
                    for i in range(4):
                        last = pe.transpose(dst[:, side * G + i * P:side * G + (i + 1) * P],
                                            skp[:, side, 4 * c + i, :], ident[:, :])
                    if side == 0:
                        yield
            elif kind == "W":
                s_we.wait(pe, NT * t + 4 * c + 4)
                for side in range(2):
                    for i in range(4):
                        last = pe.transpose(dst[:, side * G + i * P:side * G + (i + 1) * P],
                                            sw[:, p % 2, 4 * c + i, (1 - side) * P:(2 - side) * P], ident[:, :])
                    if side == 0:
                        yield
            else:
                if c == 0 and j == 0:
                    s_mq.wait(pe, 16 * (t + 1))
                for e, bank in enumerate(banks(c, j)):
                    for z, lo, hi in bank:
                        last = pe.matmul(dst[:, e * G + lo:e * G + hi], zs[0:KR + NM, p % U, z * P:(z + 1) * P],
                                         qs[0:KR + NM, p % U, c * G + lo:c * G + hi], start=True, stop=True)
                    if e == 0:
                        yield
            last.then_inc(s_fl.h, 1)
            yield

        def use(pe, n, kind, c, j, t, p):
            pos = ring_static(n)
            if kind == "R":
                return
            s_cp.wait(pe, n + 1)
            src = pr[:, pos % NP, :]
            v = vs[:, p % 2, :, :]
            if kind == "F":
                if c == 0:
                    s_oev.wait(pe, 4 * t)
                if c == 2:
                    s_fa.wait(pe, 4 * t + 2)
                for side in range(2):
                    row = 32 * (2 * (c % 2) + side)
                    last = pe.matmul(psO[row:row + 32, :], ev[:, side, :], src[:, side * G:(side + 1) * G],
                                     start=True, stop=True, tile_position=(0, row))
            elif kind == "W":
                for side in range(2):
                    for i in range(4):
                        z = 4 * c + i + (0 if side == 1 else NROT)
                        last = pe.matmul(psO[32 * i:32 * i + 32, i * P:(i + 1) * P], v[:, z, :],
                                         src[:, side * G + i * P:side * G + (i + 1) * P],
                                         start=False, stop=side == 1, tile_position=(0, 32 * i),
                                         skip_group_check=True)
            else:
                if c == 0 and j == 0:
                    s_v.wait(pe, NV * (t + 1))
                    if rel:
                        s_fa.wait(pe, 4 * (t + 1))
                if j == 0:
                    s_oev.wait(pe, 4 * t + c)
                nb = 14 if rel else 16
                for e, bank in enumerate(banks(c, j)):
                    m = 2 * j + e
                    for z, lo, hi in bank:
                        q = m % 4
                        last = pe.matmul(psO[32 * q:32 * q + 32, lo:hi], v[:, z, :], src[:, e * G + lo:e * G + hi],
                                         start=m < 4, stop=not rel and m >= nb - 4, tile_position=(0, 32 * q),
                                         skip_group_check=rel)
            last.then_inc(s_us.h, 1)

        def finals(pe, t, p, c):
            if c == 0:
                if rel:
                    s_fa.wait(pe, 4 * (t + 1))
                s_oev.wait(pe, 4 * t)
                s_mr.wait(pe, t + 1)
            for i in range(4 * c, 4 * c + 4):
                last = pe.matmul(psF[:, i, :], ot[:, (p - 1) % 2, i * P:(i + 1) * P], sel[:, :],
                                 start=True, stop=True)
            if c == 3:
                last.then_inc(s_fm.h, 1)

        @blk.tensor
        def _(pe):
            s_init.wait(pe, NINIT)
            if rel:
                for n in range(RPRO):
                    for _ in fill(pe, n, "R", n % 4, 0, n // 4 - 2, None, n // 4 - 2):
                        pass
            for u in range(64):
                a_unit(pe, 0, 0, u)
            m_transpose(pe, 0)
            for u in range(EARLY):
                a_unit(pe, 1, 1, u)
            for n in range(2):
                for _ in fill(pe, At(0, n), *ring[n], 0, None, 0):
                    pass
            with pe.Fori(0, HEADS // U) as it:
                for p in range(U):
                    t = U * it + p
                    done = 0
                    for step in range(NSTEP):
                        stops = 0
                        start, new = done, banks_until(step) - done

                        def fill_banks(upto):
                            nonlocal done
                            while done < min(start + upto, start + new):
                                ahead = 1 if done < 64 - EARLY else 2
                                a_unit(pe, Head(it, p + ahead), p + ahead, (EARLY + done) % 64)
                                done += 1

                        fill_banks(A_AT[0])
                        for n in (2 * step + 2, 2 * step + 3):
                            k, n = n // NR, n % NR
                            for _ in fill(pe, At(t + k, n), *ring[n], t + k, it, p + k):
                                stops += 1
                                fill_banks(A_AT[stops])
                        assert stops == 4
                        for n in (2 * step, 2 * step + 1):
                            use(pe, At(t, n), *ring[n], t, p)
                        if step in FINALS:
                            finals(pe, t, p, FINALS.index(step))
                        if step == M_STEP:
                            m_transpose(pe, t + 1)
            if rel:
                for n in range(4):
                    if n >= 2:
                        for _ in fill(pe, At(HEADS, n), *ring[n], HEADS, None, 0):
                            pass
                    use(pe, At(HEADS, n), *ring[n], HEADS, 0)
            for c in range(4):
                finals(pe, HEADS, 0, c)
def selection(nc, ident, sel):
    with ExitStack() as ctx:
        s_sel, = sems = [ctx.enter_context(nc.semaphore(n)) for n in ("s_sel",)]
        ctx.callback(clear_semaphores, nc, sems)
        blk = ctx.enter_context(nc.Block())
        @blk.vector
        def _(dve):
            dve.reduce_sum(sel[:, :], ident[:, :].rearrange("p (j c) -> p c j", c=32), AX.X).then_inc(s_sel, 1)
            dve.wait_ge(s_sel, 1)


def rel_tables(nc, ident, emb_k, emb_v, e_stack, ev, ev_side, k_side, zero):
    with ExitStack() as ctx:
        def sb(name, shape, dt=F32):
            return ctx.enter_context(nc.sbuf_tensor("rt_" + name, shape, dt))

        ek_rows = sb("ek_rows", [P, P])
        ekt = sb("ekt", [DK, P])
        psE = ctx.enter_context(nc.psum_tensor("rt_psE", [P, P], F32))
        diff = sb("diff", [DK, W])
        rest = sb("rest", [DK, W])
        parts = sb("parts", [DK, 3, W], BF16)
        evr = sb("evr", [P, DK])
        s_ld, s_ek, s_z, s_e, s_st = sems = [ctx.enter_context(nc.semaphore("rt_" + n)) for n in
                                             ("s_ld", "s_ek", "s_z", "s_e", "s_st")]
        ctx.callback(clear_semaphores, nc, sems)
        blk = ctx.enter_context(nc.Block())

        @blk.sync
        def _(sp):
            sp.wait_ge(s_ek, 1)
            sp.dma_start(ek_rows[:, 0:DK], emb_k[0:P, :]).then_inc(s_ek, 16)
            sp.dma_start(evr[:, :], emb_v[0:P, :]).then_inc(s_ld, 16)
            for side, r in ((0, 0), (1, 2 * MRP)):
                row = emb_v[r:r + 1, :]
                sp.dma_start(ev_side[:, side, :, :], bass.AP(row.tensor, row.offset, [[0, P], [0, NROT], [1, DK]])
                             ).then_inc(s_ld, 16)
                for hh in range(P // DK):
                    sp.dma_start(k_side[hh * DK:(hh + 1) * DK, side:side + 1],
                                 emb_k[r:r + 1, :].rearrange("r (d a) -> (r d) a", a=1)).then_inc(s_ld, 16)
            sp.wait_ge(s_e, 10)
            for i, part in enumerate(K_PART):
                sp.dma_start(e_stack[i * DK:(i + 1) * DK, :], parts[:, part, :]).then_inc(s_st, 16)
            sp.wait_ge(s_st, 16 * len(K_PART))

        @blk.vector
        def _(dve):
            dve.memset(ek_rows[:, DK:P], 0.0).then_inc(s_ek, 1)
            dve.memset(zero[:, :], 0.0).then_inc(s_z, 1)
            dve.wait_ge(s_z, 1)
            n = [0]

            def then(ins, wait=True):
                n[0] += 1
                ins.then_inc(s_e, 1)
                if wait:
                    dve.wait_ge(s_e, n[0])

            then(dve.memset(ev[:, :, :], 0.0))
            dve.wait_ge(s_ek, 18)
            then(dve.tensor_copy(ekt[:, :], psE[0:DK, :]))
            dve.wait_ge(s_ld, 16 * (3 + 2 * P // DK))
            for side in range(2):
                then(dve.tensor_scalar(diff[:, side * P:(side + 1) * P], ekt[:, :], k_side[0:DK, side:side + 1],
                                       None, ALU.subtract), wait=False)
                then(dve.tensor_tensor(out=ev[:, side, 0:DK], in0=evr[:, :], in1=ev_side[:, side, 0, :],
                                       op=ALU.subtract))
            then(dve.tensor_copy(parts[:, 0, :], diff[:, :]))
            then(dve.tensor_tensor(out=rest[:, :], in0=diff[:, :], in1=parts[:, 0, :], op=ALU.subtract))
            then(dve.tensor_copy(parts[:, 1, :], rest[:, :]))
            then(dve.tensor_tensor(out=parts[:, 2, :], in0=rest[:, :], in1=parts[:, 1, :], op=ALU.subtract))

        @blk.tensor
        def _(pe):
            pe.wait_ge(s_ek, 17)
            pe.transpose(psE[:, :], ek_rows[:, :], ident[:, :]).then_inc(s_ek, 1)


def load_small(nc, name, pairs, adds=()):
    with ExitStack() as ctx:
        s_ld, s_add = sems = [ctx.enter_context(nc.semaphore(n)) for n in (name + "_ld", name + "_add")]
        ctx.callback(clear_semaphores, nc, sems)
        blk = ctx.enter_context(nc.Block())
        @blk.sync
        def _(sp):
            with nc.allow_non_contiguous_dma(reason="small vectors, once"):
                for dst, src in pairs:
                    sp.dma_start(dst, src).then_inc(s_ld, 16)
            sp.wait_ge(s_ld, 16 * len(pairs))

        @blk.vector
        def _(dve):
            if adds:
                dve.wait_ge(s_ld, 16 * len(pairs))
                for out, a, b in adds:
                    dve.tensor_tensor(out=out, in0=a, in1=b, op=ALU.add).then_inc(s_add, 1)
                dve.wait_ge(s_add, len(adds))


def out_stage(nc, tag, o_rows, wo, bo, resid, dst, ident):
    with ExitStack() as ctx:
        def sb(name, shape, dt=F32):
            return ctx.enter_context(nc.sbuf_tensor(f"{tag}_{name}", shape, dt))

        sems = []

        def sem(name, credit=32):
            sems.append(Sem(ctx, nc, f"{tag}_{name}", credit))
            return sems[-1]

        res = sb("res", [P, 2, TPG, D])
        rb = sb("rb", [P, 2, TPG, D])
        y = sb("y", [P, 2, TPG, D])
        ot = sb("ot", [P, 2, CH, G])
        os = sb("os", [P, 2, TPG, D])
        psT = ctx.enter_context(nc.psum_tensor(f"{tag}_psT", [P, CH, G], F32))
        psY = ctx.enter_context(nc.psum_tensor(f"{tag}_psY", [P, 2, 2, D], F32))
        s_ld = [sem(f"s_ld{i}") for i in range(2)]
        s_st = [sem(f"s_st{i}") for i in range(2)]
        s_os = [sem(f"s_os{i}") for i in range(2)]
        s_rb, s_t, s_ot, s_y, s_yo = (sem(n) for n in ("s_rb", "s_t", "s_ot", "s_y", "s_yo"))
        ctx.callback(clear_semaphores, nc, sems)
        blk = ctx.enter_context(nc.Block())
        rv = resid.rearrange("(g j p) c -> g p j c", p=P, j=TPG)
        ov = o_rows.rearrange("(g j p) c -> g p j c", p=P, j=TPG)
        dv = dst.rearrange("(g j p) c -> g p j c", p=P, j=TPG)

        @blk.sync
        def _(sp):
            give_credits(sp, sems)
            with sp.Fori(0, NG // 2) as it:
                for q in range(2):
                    g = 2 * it + q
                    wait_all(sp, (s_rb, g - 1),
                             (s_t, CH * (g - 1)))
                    sp.dma_start(os[:, q, :, :], ov[bass.ds(g, 1), :, :, :].rearrange("g p j c -> p (g j) c")
                                 ).then_inc(s_os[q].h, 16)
                    sp.dma_start(res[:, q, :, :], rv[bass.ds(g, 1), :, :, :].rearrange("g p j c -> p (g j) c")
                                 ).then_inc(s_ld[q].h, 16)

        @blk.gpsimd
        def _(pool):
            with pool.Fori(0, NG // 2) as it:
                for q in range(2):
                    g = 2 * it + q
                    s_ld[q].wait(pool, 16 * (it + 1))
                    s_yo.wait(pool, 2 * (g - 1))
                    pool.tensor_tensor(out=rb[:, q, :, :], in0=res[:, q, :, :],
                                       in1=bo[:, :].rearrange("p (a c) -> p a c", a=1).to_broadcast([P, TPG, D]),
                                       op=ALU.add).then_inc(s_rb.h, 1)

        @blk.tensor
        def _(pe):
            with pe.Fori(0, NG // 2) as it:
                for q in range(2):
                    g = 2 * it + q
                    s_os[q].wait(pe, 16 * (it + 1))
                    for c in range(CH):
                        s_ot.wait(pe, CH * (g - 1) + c + 1)
                        for j in range(TPG):
                            last = pe.transpose(psT[:, c, j * P:(j + 1) * P],
                                                os[:, q, j, c * P:(c + 1) * P], ident[:, :])
                        last.then_inc(s_t.h, 1)
                    s_ot.wait(pe, CH * (g + 1))
                    for v in range(2):
                        s_yo.wait(pe, 2 * (g - 1) + v + 1)
                        for i in range(2):
                            for c in range(CH):
                                j = 2 * v + i
                                last = pe.matmul(psY[:, v, i, :], ot[:, q, c, j * P:(j + 1) * P], wo[:, c, :],
                                                 start=c == 0, stop=c == CH - 1)
                        last.then_inc(s_y.h, 1)

        @blk.scalar
        def _(act):
            with act.Fori(0, NG // 2) as it:
                for q in range(2):
                    g = 2 * it + q
                    for c in range(CH):
                        s_t.wait(act, CH * g + c + 1)
                        if c == 0:
                            s_y.wait(act, 2 * (g - 1))
                        act.activation(ot[:, q, c, :], psT[:, c, :], ACT.Copy).then_inc(s_ot.h, 1)
                    s_yo.wait(act, 2 * (g + 1))
                    act.dma_start(dv[bass.ds(g, 1), :, :, :].rearrange("g p j c -> p (g j) c"), y[:, q, :, :]
                                  ).then_inc(s_st[q].h, 16)
            for q in range(2):
                s_st[q].wait(act, 16 * NG // 2)

        @blk.vector
        def _(dve):
            with dve.Fori(0, NG // 2) as it:
                for q in range(2):
                    g = 2 * it + q
                    s_rb.wait(dve, g + 1)
                    s_st[q].wait(dve, 16 * it)
                    for v in range(2):
                        s_y.wait(dve, 2 * g + v + 1)
                        dve.tensor_tensor(out=y[:, q, 2 * v:2 * v + 2, :], in0=psY[:, v, :, :],
                                          in1=rb[:, q, 2 * v:2 * v + 2, :], op=ALU.add).then_inc(s_yo.h, 1)


def routing(nc, lg, gb, ew, ew_t, b1_dram, b1_t, ident, x1, f2, acc):
    TT = T // P
    with ExitStack() as ctx:
        def sb(name, shape, dt=F32):
            return ctx.enter_context(nc.sbuf_tensor("ro_" + name, shape, dt))

        top = sb("top", [P, TT, 8])
        idx = sb("idx", [P, TT, 8], mybir.dt.uint32)
        idf = sb("idf", [P, TT, 2])
        number = sb("number", [P, NE])
        dif, ex, den, w = sb("dif", [P, TT]), sb("ex", [P, TT]), sb("den", [P, TT]), sb("w", [P, TT, 2])
        hot = sb("hot", [P, 2, TT, NE])
        b1r = sb("b1r", [NE * FC, P])
        a_in = sb("a_in", [P, 2, TPG, D])
        b_in = sb("b_in", [P, 2, TPG, D])
        psE = ctx.enter_context(nc.psum_tensor("ro_psE", [P, TT * P], F32))
        s_n, s_lg, s_top, s_i, s_v, s_ex, s_b, s_t, s_o, s_in0, s_in1, s_xf = sems = [
            ctx.enter_context(nc.semaphore("ro_" + n)) for n in
            ("s_n", "s_lg", "s_top", "s_i", "s_v", "s_ex", "s_b", "s_t", "s_o", "s_in0", "s_in1", "s_xf")]
        s_in = (s_in0, s_in1)
        ctx.callback(clear_semaphores, nc, sems)
        blk = ctx.enter_context(nc.Block())

        @blk.sync
        def _(sp):
            sp.dma_start(b1r[:, :], b1_dram.rearrange("e (f p) -> (e f) p", p=P)).then_inc(s_b, 16)
            xv = x1.rearrange("(g j p) c -> g p j c", p=P, j=TPG)
            fv = f2.rearrange("(g j p) c -> g p j c", p=P, j=TPG)
            for g in range(NG):
                if g >= 2:
                    sp.wait_ge(s_xf, g - 1)
                sp.dma_start(a_in[:, g % 2, :, :], xv[g]).then_inc(s_in[g % 2], 16)
                sp.dma_start(b_in[:, g % 2, :, :], fv[g]).then_inc(s_in[g % 2], 16)

        @blk.gpsimd
        def _(pool):
            for e in range(NE):
                pool.memset(number[:, e:e + 1], float(e)).then_inc(s_n, 1)
            for g in range(NG):
                pool.wait_ge(s_in[g % 2], 32 * (g // 2 + 1))
                pool.tensor_tensor(out=acc[:, g * TPG:(g + 1) * TPG, :], in0=a_in[:, g % 2, :, :],
                                   in1=b_in[:, g % 2, :, :], op=ALU.add).then_inc(s_xf, 1)
            pool.wait_ge(s_xf, NG)

        @blk.scalar
        def _(act):
            act.wait_ge(s_v, 2)
            act.activation(ex[:, :], dif[:, :], ACT.Exp).then_inc(s_ex, 1)

        @blk.vector
        def _(dve):
            dve.tensor_tensor(out=lg[:, :, :], in0=lg[:, :, :],
                              in1=gb[:, :].rearrange("p (a e) -> p a e", a=1).to_broadcast([P, TT, NE]),
                              op=ALU.add).then_inc(s_lg, 1)
            dve.wait_ge(s_lg, 1)
            for j in range(TT):
                dve.max(out=top[:, j, :], in_=lg[:, j, :]).then_inc(s_top, 1)
            for j in range(TT):
                dve.wait_ge(s_top, j + 1)
                dve.max_index(idx[:, j, :], top[:, j, :], lg[:, j, :]).then_inc(s_i, 1)
            dve.wait_ge(s_i, TT)
            n = [0]

            def then(ins, wait=True):
                n[0] += 1
                ins.then_inc(s_v, 1)
                if wait:
                    dve.wait_ge(s_v, n[0])

            then(dve.tensor_copy(idf[:, :, :], idx[:, :, 0:2]))
            then(dve.tensor_tensor(out=dif[:, :], in0=top[:, :, 1], in1=top[:, :, 0], op=ALU.subtract))
            dve.wait_ge(s_ex, 1)
            then(dve.tensor_scalar_add(den[:, :], ex[:, :], 1.0))
            then(dve.reciprocal(w[:, :, 0], den[:, :]))
            then(dve.tensor_tensor(out=w[:, :, 1], in0=ex[:, :], in1=w[:, :, 0], op=ALU.mult))
            dve.wait_ge(s_n, NE)
            for k in range(2):
                then(dve.tensor_tensor(out=hot[:, k, :, :], in0=number[:, :].rearrange("p (a e) -> p a e", a=1
                                       ).to_broadcast([P, TT, NE]),
                                       in1=idf[:, :, k:k + 1].to_broadcast([P, TT, NE]), op=ALU.is_equal))
                then(dve.tensor_tensor(out=hot[:, k, :, :], in0=hot[:, k, :, :],
                                       in1=w[:, :, k:k + 1].to_broadcast([P, TT, NE]), op=ALU.mult))
            then(dve.tensor_tensor(out=ew[:, :, :], in0=hot[:, 0, :, :], in1=hot[:, 1, :, :], op=ALU.add))
            dve.wait_ge(s_t, 1)
            dve.tensor_copy(b1_t[:, :], psE[:, 0:NE * FC]).then_inc(s_o, 1)
            dve.wait_ge(s_t, 2)
            dve.tensor_copy(ew_t[:, :], psE[0:NE, :]).then_inc(s_o, 1)
            dve.wait_ge(s_o, 2)

        @blk.tensor
        def _(pe):
            pe.wait_ge(s_b, 16)
            pe.transpose(psE[:, 0:NE * FC], b1r[:, :], ident[0:NE * FC, 0:NE * FC]).then_inc(s_t, 1)
            pe.wait_ge(s_v, 10)
            pe.wait_ge(s_o, 1)
            for j in range(TT):
                last = pe.transpose(psE[0:NE, j * P:(j + 1) * P], ew[:, j, :], ident[:, :])
            last.then_inc(s_t, 1)


PARTS = ((0, 0), (0, 1), (1, 0))


def moe_stage(nc, hT, ew, ew_t, w1, b1_t, w2, b2_sb, acc, out):
    TT = T // P
    F32R = mybir.dt.float32r
    NHID = 4
    with ExitStack() as ctx:
        def sb(name, shape, dt=F32):
            return ctx.enter_context(nc.sbuf_tensor("mo_" + name, shape, dt))

        sems = []

        def sem(name, credit=256):
            sems.append(Sem(ctx, nc, "mo_" + name, credit))
            return sems[-1]

        raw = [sb("w1_raw", [P, CH, DFF]), sb("w2_raw", [P, FC, D])]
        wp = [sb("w1_parts", [P, 2, 2, CH, DFF], F32R), sb("w2_parts", [P, 2, 2, FC, D], F32R)]
        hp = sb("h_parts", [P, 2, 2, CH, G], F32R)
        whole = sb("hid", [P, NHID, G])
        hid = sb("hid_parts", [P, 2, NHID, G], F32R)
        b1_now = sb("b1_now", [P, 2, FC])
        psH = ctx.enter_context(nc.psum_tensor("mo_psH", [P, 4, G], F32))
        psY = ctx.enter_context(nc.psum_tensor("mo_psY", [P, 4, G], F32))
        s_raw = [sem(f"s_raw{k}") for k in range(2)]
        s_w0, s_w1 = sem("s_w0"), sem("s_w1")
        s_hs = sem("s_hs")
        s_h, s_r, s_lo = sem("s_h"), sem("s_r"), sem("s_lo")
        s_l2 = sem("s_l2")
        s_y, s_acc, s_0, s_b, s_b1, s_out = (sem(n) for n in ("s_y", "s_acc", "s_0", "s_b", "s_b1", "s_out"))
        ctx.callback(clear_semaphores, nc, sems)
        blk = ctx.enter_context(nc.Block())

        def load_w(sp, e):
            row = ready(sp, e % NE)
            for k, src in enumerate((w1[bass.ds(row, 1), :, :].rearrange("e (c p) f -> p (e c) f", p=P),
                                     w2[bass.ds(row, 1), :, :].rearrange("e (f p) d -> p (e f) d", p=P))):
                s_w1.wait(sp, 2 * (e - 1) + k + 1)
                sp.dma_start(raw[k][:, :, :], src).then_inc(s_raw[k].h, 16)

        def chunk_used(eng, n, f):
            if f < 0:
                n, f = n - 1, f + FC
            if f < FC - 1:
                s_l2.wait(eng, (FC - 1) * n + f + 1)
            else:
                s_y.wait(eng, TPG * (n + 1))

        @blk.sync
        def _(sp):
            give_credits(sp, sems)
            load_w(sp, 0)
            with sp.Fori(1, NE + 1) as e:
                load_w(sp, e)
            s_acc.wait(sp, TT * NE)
            sp.dma_start(out.rearrange("(j p) c -> p j c", p=P), acc[:, :, :]).then_inc(s_out.h, 16)
            s_out.wait(sp, 16)

        @blk.gpsimd
        def _(pool):
            with pool.Fori(0, NE // 2) as it:
                for q in range(2):
                    e = 2 * it + q
                    for k in range(2):
                        s_w0.wait(pool, 2 * e + k + 1)
                        pool.tensor_tensor(out=wp[k][:, q, 1, :, :], in0=raw[k][:, :, :],
                                           in1=wp[k][:, q, 0, :, :], op=ALU.subtract).then_inc(s_w1.h, 1)

        @blk.tensor
        def _(pe):
            for j in range(TT):
                s_b.wait(pe, j - 3)
                pe.matmul(psY[:, j % 4, 0:D], ew_t[:, j * P:(j + 1) * P], b2_sb[:, :], start=True, stop=True
                          ).then_inc(s_0.h, 1)
            s_b.wait(pe, TT)

            def first(n, q, r, f):
                s_r.wait(pe, 2 * (FC * n + f - 3))
                for c in range(CH):
                    for m, (a, b) in enumerate(PARTS):
                        last = pe.matmul(psH[:, f % 4, :], wp[0][:, q, a, c, f * P:(f + 1) * P],
                                         hp[:, r, b, c, :], start=c == 0 and m == 0,
                                         stop=c == CH - 1 and m == len(PARTS) - 1)
                last.then_inc(s_h.h, 1)

            def second(n, q, f):
                s_lo.wait(pe, FC * n + f + 1)
                for j in range(TPG):
                    if f == 0:
                        s_acc.wait(pe, TPG * (n - 1) + j + 1)
                    for m, (a, b) in enumerate(PARTS):
                        last = pe.matmul(psY[:, j, 0:D], hid[:, a, f % NHID, j * P:(j + 1) * P],
                                         wp[1][:, q, b, f, :], start=f == 0 and m == 0,
                                         stop=f == FC - 1 and m == len(PARTS) - 1)
                    if f == FC - 1:
                        last.then_inc(s_y.h, 1)
                if f < FC - 1:
                    last.then_inc(s_l2.h, 1)

            with pe.Fori(0, NE // 2) as it:
                for q in range(2):
                    with pe.Fori(0, NG // 2) as gg:
                        for r in range(2):
                            e = 2 * it + q
                            n = e * NG + 2 * gg + r
                            s_w1.wait(pe, 2 * (e + 1))
                            s_hs.wait(pe, 2 * (n + 1))
                            for f in range(-2, FC):
                                if f + 2 < FC:
                                    first(n, q, r, f + 2)
                                if f >= 0:
                                    second(n, q, f)

        @blk.scalar
        def _(act):
            with act.Fori(0, NE // 2) as it:
                for q in range(2):
                    with act.Fori(0, NG // 2) as gg:
                        for r in range(2):
                            e = 2 * it + q
                            n = e * NG + 2 * gg + r
                            s_b1.wait(act, e + 1)
                            for f in range(FC):
                                u = FC * n + f
                                s_h.wait(act, u + 1)
                                s_lo.wait(act, u - NHID + 1)
                                chunk_used(act, n, f - NHID)
                                for dst in (whole[:, f % NHID, :], hid[:, 0, f % NHID, :]):
                                    act.activation(dst, psH[:, f % 4, :], ACT.Relu, bias=b1_now[:, q, f:f + 1]
                                                   ).then_inc(s_r.h, 1)

        def split_h(dve, n, g, r):
            s_h.wait(dve, FC * (n - 1))
            src = hT[:, :, bass.ds(g * G, G)]
            dve.tensor_copy(hp[:, r, 0, :, :], src).then_inc(s_hs.h, 1)
            s_hs.wait(dve, 2 * n + 1)
            dve.tensor_tensor(out=hp[:, r, 1, :, :], in0=src, in1=hp[:, r, 0, :, :], op=ALU.subtract
                              ).then_inc(s_hs.h, 1)

        def round_w(dve, e, q):
            for k in range(2):
                s_raw[k].wait(dve, 16 * (e + 1))
                s_y.wait(dve, TT * (e - 1))
                dve.tensor_copy(wp[k][:, q, 0, :, :], raw[k][:, :, :]).then_inc(s_w0.h, 1)

        @blk.vector
        def _(dve):
            for j in range(TT):
                s_0.wait(dve, j + 1)
                dve.tensor_tensor(out=acc[:, j, :], in0=psY[:, j % 4, 0:D], in1=acc[:, j, :], op=ALU.add
                                  ).then_inc(s_b.h, 1)
            s_b.wait(dve, TT)
            round_w(dve, 0, 0)
            split_h(dve, 0, 0, 0)
            with dve.Fori(0, NE // 2) as it:
                for q in range(2):
                    s_r.wait(dve, 2 * FC * NG * (2 * it + q - 1))
                    dve.tensor_copy(b1_now[:, q, :], b1_t[:, bass.ds((2 * it + q) * FC, FC)]).then_inc(s_b1.h, 1)
                    round_w(dve, 2 * it + q + 1, 1 - q)
                    with dve.Fori(0, NG // 2) as gg:
                        for r in range(2):
                            e = 2 * it + q
                            g = 2 * gg + r
                            n = e * NG + g
                            for f in range(FC):
                                if f == 2:
                                    split_h(dve, n + 1, g + 1 if r == 0 else (g + 1) % NG, 1 - r)
                                s_r.wait(dve, 2 * (FC * n + f + 1))
                                chunk_used(dve, n, f - NHID)
                                dve.tensor_tensor(out=hid[:, 1, f % NHID, :], in0=whole[:, f % NHID, :],
                                                  in1=hid[:, 0, f % NHID, :], op=ALU.subtract).then_inc(s_lo.h, 1)
                            s_acc.wait(dve, TPG * (n - (NG - 1)))
                            for j in range(TPG):
                                s_y.wait(dve, TPG * n + j + 1)
                                row = acc[:, bass.ds(g * TPG + j, 1), :].rearrange("p a c -> p (a c)")
                                dve.scalar_tensor_tensor(
                                    out=row, in0=psY[:, j, 0:D],
                                    scalar=ew[:, bass.ds(g * TPG + j, 1), bass.ds(e, 1)].rearrange("p a e -> p (a e)"),
                                    in1=row, op0=ALU.mult, op1=ALU.add).then_inc(s_acc.h, 1)


def program(nc, A, out):
    def dram(name, shape, dt=F32):
        return nc.dram_tensor(name, shape, dt).ap()

    q_parts, kl_parts, kr_parts = (dram(n, (3, D, T), BF16) for n in ("q_parts", "kl_parts", "kr_parts"))
    v_rows, o_rows, x1, f_rows, f2_rows = (dram(n, (T, D)) for n in
                                           ("v_rows", "o_rows", "x1_rows", "f_rows", "f2_rows"))
    tables = dram("skewed_tables", (NG, NT, P, W))
    dr_r, dr_p = (tables[4 * n:4 * n + 4].rearrange("(a b) i q r -> a b i q r", a=2) for n in range(2))

    def column(vec, c):
        return vec[c * P:(c + 1) * P].rearrange("(p a) -> p a", a=1)

    with ExitStack() as top:
        def sb(stack, name, shape, dt=F32):
            return stack.enter_context(nc.sbuf_tensor(name, shape, dt))

        ident = sb(top, "ident", [P, P])
        sel = sb(top, "sel", [P, 32])
        ident_and_ones(nc, ident)
        selection(nc, ident, sel)

        with ExitStack() as one:
            e_stack = sb(one, "e_stack", [P, W], BF16)
            ev = sb(one, "ev", [P, 2, 32])
            ev_side = sb(one, "ev_side", [P, 2, NROT, DK])
            with ExitStack() as st:
                k_side = sb(st, "k_side", [P, 2])
                zero = sb(st, "zero", [P, NT * W])
                wt = sb(st, "w_qkv_t", [P, CH, 3 * D])
                cols = sb(st, "cols", [P, 8])
                vb = sb(st, "v_bias", [P, D])
                rel_tables(nc, ident, A["attn_embK"], A["attn_embV"], e_stack, ev, ev_side, k_side, zero)
                load_small(nc, "l1", [(vb[:, :], bcast_rows(A["attn_bv"]))]
                           + [(cols[:, c:c + 1], column(A["attn_bq"], c)) for c in range(CH)]
                           + [(cols[:, 2 + c:3 + c], column(A["attn_bk"], c)) for c in range(CH)],
                           [(cols[:, 4 + 2 * s + c:5 + 2 * s + c], cols[:, 2 + c:3 + c], k_side[:, s:s + 1])
                            for s in range(2) for c in range(CH)])
                for i, n in enumerate(("Wq", "Wk", "Wv")):
                    transposed_weight(nc, n + "T", A["attn_" + n], wt[:, :, i * D:(i + 1) * D], ident)
                units = [(c * P, cols[:, c:c + 1], 1.0, (q_parts, c * P)) for c in range(CH)]
                for s, dst in ((0, kl_parts), (1, kr_parts)):
                    units += [(D + c * P, cols[:, 4 + 2 * s + c:5 + 2 * s + c], 1.0, (dst, c * P)) for c in range(CH)]
                ln_proj_stage(nc, "rel", A["attn_x"], ident, wt, units, vb, {"v": v_rows},
                              zero_fill=(zero, tables))
            attention_stage(nc, True, ident, sel, q_parts, (kl_parts, kr_parts), v_rows, o_rows,
                            {"e_stack": e_stack, "ev": ev, "ev_side": ev_side, "dr_r": dr_r, "dr_p": dr_p})
            wo = sb(one, "wo_t", [P, CH, D])
            bo = sb(one, "bo", [P, D])
            load_small(nc, "o1", [(bo[:, :], bcast_rows(A["attn_bo"]))])
            transposed_weight(nc, "WoT", A["attn_Wo"], wo, ident)
            out_stage(nc, "o1", o_rows, wo, bo, A["attn_x"], x1, ident)

        with ExitStack() as two:
            with ExitStack() as st:
                wt = sb(st, "w_qkv", [P, CH, 3 * D])
                cols = sb(st, "cols2", [P, 8])
                gain = sb(st, "gain1", [P, 2, CH])
                vb = sb(st, "v_bias2", [P, D])
                load_small(nc, "l2", [(wt[:, :, :], A["ffn_w_qkv"].rearrange("(c p) n -> p c n", p=P)),
                                      (vb[:, :], bcast_rows(A["ffn_b_qkv"][2 * D:3 * D]))]
                           + [(cols[:, c:c + 1], column(A["ffn_b_qkv"], c)) for c in range(2 * CH)]
                           + [(gain[:, k, c:c + 1], column(A[n], c)) for c in range(CH)
                              for k, n in enumerate(("ffn_ln1_g", "ffn_ln1_b"))])
                units = [(c * P, cols[:, c:c + 1], float(DK) ** -0.5, (q_parts, c * P)) for c in range(CH)]
                units += [(D + c * P, cols[:, 2 + c:3 + c], 1.0, (kl_parts, c * P)) for c in range(CH)]
                ln_proj_stage(nc, "plain", x1, ident, wt, units, vb, {"v": v_rows}, gain=gain, save_ln=f_rows)
            attention_stage(nc, False, ident, sel, q_parts, (kl_parts, None), v_rows, o_rows)
            wo = sb(two, "wo2", [P, CH, D])
            bo = sb(two, "bo2", [P, D])
            load_small(nc, "o2", [(bo[:, :], bcast_rows(A["ffn_b_o"])),
                                  (wo[:, :, :], A["ffn_w_o"].rearrange("(c p) n -> p c n", p=P))])
            out_stage(nc, "o2", o_rows, wo, bo, f_rows, f2_rows, ident)

        with ExitStack() as three:
            hT = sb(three, "hT_all", [P, CH, T])
            lg = sb(three, "gate_logits", [P, T // P, NE])
            ew = sb(three, "ew", [P, T // P, NE])
            ew_t = sb(three, "ew_t", [NE, T])
            b1_t = sb(three, "b1_t", [P, NE * FC])
            b2_sb = sb(three, "b2_sb", [NE, D])
            acc = sb(three, "acc", [P, T // P, D])
            with ExitStack() as st:
                gate = sb(st, "gate", [P, CH, NE])
                gain = sb(st, "gain2", [P, 2, CH])
                gb = sb(st, "gate_bias", [P, NE])
                load_small(nc, "l3", [(gate[:, :, :], A["ffn_gate_w"].rearrange("(c p) e -> p c e", p=P)),
                                      (gb[:, :], bcast_rows(A["ffn_gate_b"])), (b2_sb[:, :], A["ffn_b2"])]
                           + [(gain[:, k, c:c + 1], column(A[n], c)) for c in range(CH)
                              for k, n in enumerate(("ffn_ln2_g", "ffn_ln2_b"))])
                ln_proj_stage(nc, "gate", f2_rows, ident, None, [], None,
                              {"hT_all": hT, "gate": gate, "logits": lg}, gain=gain)
                routing(nc, lg, gb, ew, ew_t, A["ffn_b1"], b1_t, ident, x1, f2_rows, acc)
            moe_stage(nc, hT, ew, ew_t, A["ffn_W1"], b1_t, A["ffn_W2"], b2_sb, acc, out)


def kernel(**inputs):
    import numpy as _np
    import concourse.bacc as _bacc
    from concourse import mybir as _mybir
    from concourse.bass_utils import run_bass_kernel_spmd as _run

    nc = _bacc.Bacc("TRN2", target_bir_lowering=False, num_devices=1)
    arrays, args = {}, {}
    for name, value in inputs.items():
        if name == "L0_attn_mask":
            continue
        a = _np.ascontiguousarray(value)
        if name == "L0_attn_x":
            a = a.reshape(T, D)
        short = name[3:]
        arrays[short] = a
        args[short] = nc.dram_tensor(short, a.shape, _mybir.dt.from_np(a.dtype), kind="ExternalInput").ap()
    out = nc.dram_tensor("out", (T, D), _mybir.dt.float32, kind="ExternalOutput").ap()
    program(nc, args, out)
    r = _run(nc, [arrays], core_ids=[0])
    return r.results[0]["out"].reshape(NB, S, D)
```
